# Optimizing a Trainium2 kernel written in Bass

```python
import numpy as np
import jax
import jax.numpy as jnp

def _softmax(x, axis=-1):
    return jax.nn.softmax(x, axis=axis)

def _gelu(x):
    return jax.nn.gelu(x, approximate=True)

def _silu(x):
    return jax.nn.silu(x)

def _sigmoid(x):
    return jax.nn.sigmoid(x)

def _layernorm(x, axis=-1, eps=1e-05):
    m = jnp.mean(x, axis=axis, keepdims=True)
    v = jnp.var(x, axis=axis, keepdims=True)
    return (x - m) / jnp.sqrt(v + eps)

def _scatter_add(tgt, idx, src, axis=0):
    return tgt.at[idx].add(src)

def _segment_sum(src, seg, n):
    return jax.ops.segment_sum(src, seg, n)
kernel_name = 'mk_vit_tower_cls_d1_tok_img512_r4_0b619e'

def setup_inputs(seed: int=0):
    np.random.seed(seed)
    _w = jnp.asarray

    def _rec_inputs():
        import jax
        import jax.numpy as jnp
        _rk = jax.random.key(seed)
        x = -0.000392918 + 0.999932 * jax.random.normal(jax.random.fold_in(_rk, 1), (8, 1, 128, 128), jnp.float32)
        cls_tok = 0.02 * jax.random.normal(jax.random.fold_in(_rk, 5), (1, 1, 128), jnp.float32)
        return (x, cls_tok)
    x, cls_tok = _rec_inputs()

    def _L0_tok_setup():
        import math
        import jax, jax.numpy as jnp
        import numpy as np
        PW = PH = 16
        EMB = 128
        HID = 128
        B, H, W = (64, 128, 128)
        L = H // PW * (W // PH)
        SIGMA_ZERO = 0.1

        def _f_noise(x):
            return jnp.sign(x) * jnp.sqrt(jnp.abs(x))

        def _noisy_linear(x, w, b, sw, sb, eps_in, eps_out):
            ei = _f_noise(eps_in)
            eo = _f_noise(eps_out)
            w_n = w + sw * (eo[:, None] * ei[None, :])
            b_n = b + sb * eo
            return x @ w_n.T + b_n

        def _unfold_patches(x):
            b = x.shape[0]
            p = x.reshape(b, H // PW, PW, W // PH, PH)
            p = p.transpose(0, 1, 3, 2, 4)
            return p.reshape(b, L, PW * PH)

        def _pos_encoding(x):
            pos = jnp.arange(L, dtype=jnp.float32)[:, None]
            div = jnp.exp(jnp.arange(0, EMB, 2, dtype=jnp.float32) * (-math.log(10000.0) / EMB))
            ang = pos * div
            pe = jnp.stack([jnp.sin(ang), jnp.cos(ang)], axis=-1).reshape(L, EMB)
            return x + pe[None, :, :]
        key = jax.random.key(seed)
        ks = jax.random.split(key, 12)
        in_f = PW * PH
        sig = SIGMA_ZERO / math.sqrt(in_f)
        bnd1 = 1.0 / math.sqrt(in_f)
        bnd3 = 1.0 / math.sqrt(HID)
        u = lambda k, shape, bnd: jax.random.uniform(k, shape, jnp.float32, -bnd, bnd)
        return {'inputs': jax.random.normal(ks[0], (B, 1, H, W), jnp.float32), 'W1_w': u(ks[1], (HID, in_f), bnd1), 'W1_b': u(ks[2], (HID,), bnd1), 'W1_sw': jnp.full((HID, in_f), sig, jnp.float32), 'W1_sb': jnp.full((HID,), sig, jnp.float32), 'W2_w': u(ks[3], (HID, in_f), bnd1), 'W2_b': u(ks[4], (HID,), bnd1), 'W2_sw': jnp.full((HID, in_f), sig, jnp.float32), 'W2_sb': jnp.full((HID,), sig, jnp.float32), 'W3_w': u(ks[5], (EMB, HID), bnd3), 'W3_b': u(ks[6], (EMB,), bnd3), 'eps_in1': jax.random.normal(ks[7], (in_f,), jnp.float32), 'eps_out1': jax.random.normal(ks[8], (HID,), jnp.float32), 'eps_in2': jax.random.normal(ks[9], (in_f,), jnp.float32), 'eps_out2': jax.random.normal(ks[10], (HID,), jnp.float32)}
    _L0_tok_all = _L0_tok_setup()
    _L0_tok_in = {k: v for k, v in _L0_tok_all.items() if k in ('W1_w', 'W1_b', 'W1_sw', 'W1_sb', 'W2_w', 'W2_b', 'W2_sw', 'W2_sb', 'W3_w', 'W3_b', 'eps_in1', 'eps_out1', 'eps_in2', 'eps_out2')}
    del _L0_tok_all

    def _L0_attn_setup():
        import jax, jax.numpy as jnp
        import numpy as np
        NUM_HEAD = 8
        DIM_MODEL = 128
        DIM_HEAD = DIM_MODEL // NUM_HEAD
        LN_EPS = 1e-05
        key = jax.random.key(seed)
        ks = jax.random.split(key, 12)
        B, L, D = (4, 512, DIM_MODEL)
        s = 0.02
        return {'x': jax.random.normal(ks[0], (B, L, D), dtype=jnp.float32), 'Wq': jax.random.normal(ks[1], (D, D), dtype=jnp.float32) * s, 'bq': jnp.zeros((D,), dtype=jnp.float32), 'Wk': jax.random.normal(ks[2], (D, D), dtype=jnp.float32) * s, 'bk': jnp.zeros((D,), dtype=jnp.float32), 'Wv': jax.random.normal(ks[3], (D, D), dtype=jnp.float32) * s, 'bv': jnp.zeros((D,), dtype=jnp.float32), 'Wo': jax.random.normal(ks[4], (D, D), dtype=jnp.float32) * s, 'bo': jnp.zeros((D,), dtype=jnp.float32), 'gamma': jnp.ones((D,), dtype=jnp.float32), 'beta': jnp.zeros((D,), dtype=jnp.float32)}
    _L0_attn_all = _L0_attn_setup()
    _L0_attn_in = {k: v for k, v in _L0_attn_all.items() if k in ('Wq', 'bq', 'Wk', 'bk', 'Wv', 'bv', 'Wo', 'bo', 'gamma', 'beta')}
    del _L0_attn_all

    def _L0_ffn_setup():
        import jax, jax.numpy as jnp
        import numpy as np
        B, T, C = (8, 256, 128)
        H = 256
        G, EG = (2, 4)
        E = G * EG
        K = 2
        LN_EPS = 1e-05

        def _swiglu(x):
            a, b = jnp.split(x, 2, axis=-1)
            return jax.nn.silu(a) * b
        key = jax.random.key(seed)
        ks = jax.random.split(key, 8)
        n = lambda k, shape, s: jax.random.normal(k, shape, dtype=jnp.float32) * s
        return {'x': n(ks[0], (B, T, C), 1.0), 'ln_scale': jnp.ones((C,), jnp.float32), 'ln_bias': jnp.zeros((C,), jnp.float32), 'shared_in_w': n(ks[1], (2 * H, C), 0.02), 'shared_out_w': n(ks[2], (C, H), 0.02), 'shared_out_b': jnp.zeros((C,), jnp.float32), 'expert_in_w': n(ks[3], (2 * H, C), 0.02), 'expert_out_weight': n(ks[4], (E, C, H), 0.02), 'expert_out_bias': jnp.zeros((E, C), jnp.float32), 'group_gate_w': n(ks[5], (G, C), 0.02), 'expert_gate_w': n(ks[6], (E, C), 0.02), 'group_bias': jnp.zeros((G,), jnp.float32), 'expert_bias': jnp.zeros((E,), jnp.float32)}
    _L0_ffn_all = _L0_ffn_setup()
    _L0_ffn_in = {k: v for k, v in _L0_ffn_all.items() if k in ('ln_scale', 'ln_bias', 'shared_in_w', 'shared_out_w', 'shared_out_b', 'expert_in_w', 'expert_out_weight', 'expert_out_bias', 'group_gate_w', 'expert_gate_w', 'group_bias', 'expert_bias')}
    del _L0_ffn_all
    return {'x': x, 'cls_tok': cls_tok, 'L0_tok_W1_w': _L0_tok_in['W1_w'], 'L0_tok_W1_b': _L0_tok_in['W1_b'], 'L0_tok_W1_sw': _L0_tok_in['W1_sw'], 'L0_tok_W1_sb': _L0_tok_in['W1_sb'], 'L0_tok_W2_w': _L0_tok_in['W2_w'], 'L0_tok_W2_b': _L0_tok_in['W2_b'], 'L0_tok_W2_sw': _L0_tok_in['W2_sw'], 'L0_tok_W2_sb': _L0_tok_in['W2_sb'], 'L0_tok_W3_w': _L0_tok_in['W3_w'], 'L0_tok_W3_b': _L0_tok_in['W3_b'], 'L0_tok_eps_in1': _L0_tok_in['eps_in1'], 'L0_tok_eps_out1': _L0_tok_in['eps_out1'], 'L0_tok_eps_in2': _L0_tok_in['eps_in2'], 'L0_tok_eps_out2': _L0_tok_in['eps_out2'], 'L0_attn_Wq': _L0_attn_in['Wq'], 'L0_attn_bq': _L0_attn_in['bq'], 'L0_attn_Wk': _L0_attn_in['Wk'], 'L0_attn_bk': _L0_attn_in['bk'], 'L0_attn_Wv': _L0_attn_in['Wv'], 'L0_attn_bv': _L0_attn_in['bv'], 'L0_attn_Wo': _L0_attn_in['Wo'], 'L0_attn_bo': _L0_attn_in['bo'], 'L0_attn_gamma': _L0_attn_in['gamma'], 'L0_attn_beta': _L0_attn_in['beta'], 'L0_ffn_ln_scale': _L0_ffn_in['ln_scale'], 'L0_ffn_ln_bias': _L0_ffn_in['ln_bias'], 'L0_ffn_shared_in_w': _L0_ffn_in['shared_in_w'], 'L0_ffn_shared_out_w': _L0_ffn_in['shared_out_w'], 'L0_ffn_shared_out_b': _L0_ffn_in['shared_out_b'], 'L0_ffn_expert_in_w': _L0_ffn_in['expert_in_w'], 'L0_ffn_expert_out_weight': _L0_ffn_in['expert_out_weight'], 'L0_ffn_expert_out_bias': _L0_ffn_in['expert_out_bias'], 'L0_ffn_group_gate_w': _L0_ffn_in['group_gate_w'], 'L0_ffn_expert_gate_w': _L0_ffn_in['expert_gate_w'], 'L0_ffn_group_bias': _L0_ffn_in['group_bias'], 'L0_ffn_expert_bias': _L0_ffn_in['expert_bias']}

def reference(x, cls_tok, L0_tok_W1_w, L0_tok_W1_b, L0_tok_W1_sw, L0_tok_W1_sb, L0_tok_W2_w, L0_tok_W2_b, L0_tok_W2_sw, L0_tok_W2_sb, L0_tok_W3_w, L0_tok_W3_b, L0_tok_eps_in1, L0_tok_eps_out1, L0_tok_eps_in2, L0_tok_eps_out2, L0_attn_Wq, L0_attn_bq, L0_attn_Wk, L0_attn_bk, L0_attn_Wv, L0_attn_bv, L0_attn_Wo, L0_attn_bo, L0_attn_gamma, L0_attn_beta, L0_ffn_ln_scale, L0_ffn_ln_bias, L0_ffn_shared_in_w, L0_ffn_shared_out_w, L0_ffn_shared_out_b, L0_ffn_expert_in_w, L0_ffn_expert_out_weight, L0_ffn_expert_out_bias, L0_ffn_group_gate_w, L0_ffn_expert_gate_w, L0_ffn_group_bias, L0_ffn_expert_bias):
    import jax
    import jax.numpy as jnp

    def _L0_tok_ref(inputs, W1_w, W1_b, W1_sw, W1_sb, W2_w, W2_b, W2_sw, W2_sb, W3_w, W3_b, eps_in1, eps_out1, eps_in2, eps_out2):
        import math
        import jax, jax.numpy as jnp
        import numpy as np
        PW = PH = 16
        EMB = 128
        HID = 128
        B, H, W = (64, 128, 128)
        L = H // PW * (W // PH)
        SIGMA_ZERO = 0.1

        def _f_noise(x):
            return jnp.sign(x) * jnp.sqrt(jnp.abs(x))

        def _noisy_linear(x, w, b, sw, sb, eps_in, eps_out):
            ei = _f_noise(eps_in)
            eo = _f_noise(eps_out)
            w_n = w + sw * (eo[:, None] * ei[None, :])
            b_n = b + sb * eo
            return x @ w_n.T + b_n

        def _unfold_patches(x):
            b = x.shape[0]
            p = x.reshape(b, H // PW, PW, W // PH, PH)
            p = p.transpose(0, 1, 3, 2, 4)
            return p.reshape(b, L, PW * PH)

        def _pos_encoding(x):
            pos = jnp.arange(L, dtype=jnp.float32)[:, None]
            div = jnp.exp(jnp.arange(0, EMB, 2, dtype=jnp.float32) * (-math.log(10000.0) / EMB))
            ang = pos * div
            pe = jnp.stack([jnp.sin(ang), jnp.cos(ang)], axis=-1).reshape(L, EMB)
            return x + pe[None, :, :]
        x = _unfold_patches(inputs)
        g = _noisy_linear(x, W1_w, W1_b, W1_sw, W1_sb, eps_in1, eps_out1)
        x_gate = g * jnp.tanh(jax.nn.softplus(g))
        x_inner = _noisy_linear(x, W2_w, W2_b, W2_sw, W2_sb, eps_in2, eps_out2)
        x = x_gate * x_inner
        x = x @ W3_w.T + W3_b
        return _pos_encoding(x)

    def _L0_attn_ref(x, Wq, bq, Wk, bk, Wv, bv, Wo, bo, gamma, beta):
        import jax, jax.numpy as jnp
        import numpy as np
        NUM_HEAD = 8
        DIM_MODEL = 128
        DIM_HEAD = DIM_MODEL // NUM_HEAD
        LN_EPS = 1e-05
        B, L, D = x.shape
        H, dh = (NUM_HEAD, D // NUM_HEAD)
        Q = x @ Wq.T + bq
        K = x @ Wk.T + bk
        V = x @ Wv.T + bv
        Q = Q.reshape(B * H, L, dh)
        K = K.reshape(B * H, L, dh)
        V = V.reshape(B * H, L, dh)
        scale = dh ** (-0.5)
        attn = jax.nn.softmax(jnp.einsum('bqd,bkd->bqk', Q, K) * scale, axis=-1)
        context = jnp.einsum('bqk,bkd->bqd', attn, V)
        context = context.reshape(B, L, D)
        out = context @ Wo.T + bo
        out = out + x
        mu = jnp.mean(out, axis=-1, keepdims=True)
        var = jnp.mean(jnp.square(out - mu), axis=-1, keepdims=True)
        out = (out - mu) / jnp.sqrt(var + LN_EPS) * gamma + beta
        return out

    def _L0_ffn_ref(x, ln_scale, ln_bias, shared_in_w, shared_out_w, shared_out_b, expert_in_w, expert_out_weight, expert_out_bias, group_gate_w, expert_gate_w, group_bias, expert_bias):
        import jax, jax.numpy as jnp
        import numpy as np
        B, T, C = (8, 256, 128)
        H = 256
        G, EG = (2, 4)
        E = G * EG
        K = 2
        LN_EPS = 1e-05

        def _swiglu(x):
            a, b = jnp.split(x, 2, axis=-1)
            return jax.nn.silu(a) * b
        Bx, Tx, Cx = x.shape
        S = Bx * Tx
        flat = x.reshape(S, Cx)
        mu = flat.mean(-1, keepdims=True)
        var = ((flat - mu) ** 2).mean(-1, keepdims=True)
        flat = (flat - mu) * jax.lax.rsqrt(var + LN_EPS) * ln_scale + ln_bias
        h_shared = _swiglu(flat @ shared_in_w.T)
        out_shared = h_shared @ shared_out_w.T + shared_out_b
        g_logits = flat @ group_gate_w.T + group_bias
        g_idx = jnp.argmax(g_logits, axis=-1)
        e_logits = (flat @ expert_gate_w.T).reshape(S, G, EG)
        e_sel = jnp.take_along_axis(e_logits, g_idx[:, None, None], axis=1)[:, 0, :]
        e_sel = e_sel + expert_bias.reshape(G, EG)[g_idx]
        e_probs = jax.nn.softmax(e_sel, axis=-1)
        topv, topi = jax.lax.top_k(e_probs, K)
        topv = topv / (topv.sum(-1, keepdims=True) + 1e-08)
        disp = g_idx[:, None] * EG + topi
        h_expert = _swiglu(flat @ expert_in_w.T)
        rows = jnp.arange(S)[:, None]
        comb = jnp.zeros((S, E), flat.dtype).at[rows, disp].add(topv)
        cnt = jnp.zeros((S, E), flat.dtype).at[rows, disp].add(1.0)
        routed = cnt @ expert_out_bias
        for e in range(E):
            routed = routed + comb[:, e:e + 1] * (h_expert @ expert_out_weight[e].T)
        return (out_shared + routed).reshape(Bx, Tx, Cx)
    h = _L0_tok_ref(x, L0_tok_W1_w, L0_tok_W1_b, L0_tok_W1_sw, L0_tok_W1_sb, L0_tok_W2_w, L0_tok_W2_b, L0_tok_W2_sw, L0_tok_W2_sb, L0_tok_W3_w, L0_tok_W3_b, L0_tok_eps_in1, L0_tok_eps_out1, L0_tok_eps_in2, L0_tok_eps_out2)
    h = jnp.concatenate([jnp.broadcast_to(cls_tok, (h.shape[0], 1, h.shape[2])), h], axis=1)
    h = h + _L0_attn_ref(_layernorm(h, axis=-1), L0_attn_Wq, L0_attn_bq, L0_attn_Wk, L0_attn_bk, L0_attn_Wv, L0_attn_bv, L0_attn_Wo, L0_attn_bo, L0_attn_gamma, L0_attn_beta)
    h = h + _L0_ffn_ref(_layernorm(h, axis=-1), L0_ffn_ln_scale, L0_ffn_ln_bias, L0_ffn_shared_in_w, L0_ffn_shared_out_w, L0_ffn_shared_out_b, L0_ffn_expert_in_w, L0_ffn_expert_out_weight, L0_ffn_expert_out_bias, L0_ffn_group_gate_w, L0_ffn_expert_gate_w, L0_ffn_group_bias, L0_ffn_expert_bias)
    return h

_drawn_inputs = setup_inputs


def setup_inputs(seed=0):
    import zlib

    import numpy as np

    out = dict(_drawn_inputs(seed))
    spreads = {'L0_tok_W1_sw': (0.0062500000931322575, 0.6),
     'L0_tok_W1_sb': (0.0062500000931322575, 0.6),
     'L0_tok_W2_sw': (0.0062500000931322575, 0.6),
     'L0_tok_W2_sb': (0.0062500000931322575, 0.6),
     'L0_attn_bq': (0.0, 0.8),
     'L0_attn_bk': (0.0, 0.8),
     'L0_attn_bv': (0.0, 0.638),
     'L0_attn_bo': (0.0, 0.1),
     'L0_attn_gamma': (1.0, 0.2),
     'L0_attn_beta': (0.0, 0.1),
     'L0_ffn_ln_scale': (1.0, 0.2),
     'L0_ffn_ln_bias': (0.0, 0.1),
     'L0_ffn_shared_out_b': (0.0, 0.687),
     'L0_ffn_expert_out_bias': (0.0, 0.444),
     'L0_ffn_group_bias': (0.0, 0.1),
     'L0_ffn_expert_bias': (0.0, 0.1)}
    factors = {'L0_tok_W1_b': 3.334,
     'L0_tok_W2_b': 3.34,
     'L0_attn_Wq': 8.0,
     'L0_attn_Wk': 8.0,
     'L0_attn_Wv': 4.413,
     'L0_attn_Wo': 3.901,
     'L0_ffn_shared_in_w': 8.0,
     'L0_ffn_shared_out_w': 8.0,
     'L0_ffn_expert_in_w': 8.0,
     'L0_ffn_expert_out_weight': 8.0}
    for name, (base, spread) in spreads.items():
        noise = np.random.default_rng([zlib.crc32(name.encode()), seed]).standard_normal(out[name].shape)
        drawn = base * np.exp(spread * noise) if base else spread * noise
        out[name] = jnp.asarray(drawn.astype(out[name].dtype))
    for name, factor in factors.items():
        out[name] = (out[name] * factor).astype(out[name].dtype)
    return out
```

```python
from contextlib import ExitStack

import concourse.bass as bass
from concourse import mybir

EMB = 128
IMAGES = 8
PATCHES = 64
TOKENS = PATCHES + 1
PATCH_IN = 256
K_IN = PATCH_IN // EMB
HALVES = 2
HI = IMAGES // HALVES
HP = HI * PATCHES
HT = HI * TOKENS
CHUNKS = 8
DH = EMB // CHUNKS
GROUPS = 8
UNIT = 8
UNITS = HI * GROUPS // UNIT
HID = 256
NK = HID // EMB
PAIRS = 2 * NK
EXPERTS = 8
EGROUPS = 2
EG = EXPERTS // EGROUPS
NG = EGROUPS + EXPERTS
BANK = 512
CT0 = BANK - 7 * TOKENS
SCALE = float(DH) ** -0.5
EPS = 1e-5
TOPK_EPS = 1e-8
GATE_CAP = 20.0

(C_EI1, C_EI1B, C_EI2, C_EI2B, C_EO1, C_EO2, C_B1, C_B2, C_SB1, C_SB2, C_B3, C_BQ, C_BK, C_BV, C_BO, C_GAMMA,
 C_BETA, C_LNS, C_LNB, C_SOB, C_CLS) = range(21)
NCOL = 21
NEPS = 6

F32 = mybir.dt.float32
BF16 = mybir.dt.bfloat16
ALU = mybir.AluOpType
ACT = mybir.ActivationFunctionType
AX = mybir.AxisListType
AHEAD = 1
POOL_EXPERTS = (2, 5)


def vit_tower(nc, cols, eob, patches, wtok, w3pe, stats, wqkvo, win, wso, weo, gates, gbias, ebias, sel, out):
    with ExitStack() as ctx:
        def sb(name, shape, dt=F32):
            return ctx.enter_context(nc.sbuf_tensor(name, shape, dt))

        def sem(name):
            return ctx.enter_context(nc.semaphore(name))

        cols_s = sb("cols_s", [EMB, NCOL])
        eps_in = sb("eps_in", [EMB, NEPS + 2 * EMB])
        x_s = sb("x_s", [EMB, HALVES, K_IN, HP])
        wtok_s = sb("wtok_s", [EMB, 2, 2, K_IN, EMB])
        w3pe_s = sb("w3pe_s", [EMB, EMB + PATCHES])
        stats_s = sb("stats_s", [EMB, 3, EMB])
        ident, center, mean = stats_s[:, 0, :], stats_s[:, 1, :], stats_s[:, 2, :]
        wqkvo_s = sb("wqkvo_s", [EMB, 4, EMB])
        win_s = sb("win_s", [EMB, 2, 4, EMB])
        wso_s = sb("wso_s", [EMB, NK, EMB])
        weo_s = sb("weo_s", [EMB, EXPERTS, NK, EMB])
        gates_s = sb("gates_s", [EMB, NG])
        gbias_s = sb("gbias_s", [TOKENS, NG + EG * EG])
        ebias_s = sb("ebias_s", [32, EMB])
        sel_s = sb("sel_s", [32, EXPERTS, EMB])
        selb = sb("selb", [32, EXPERTS, EMB], BF16)

        eps_t = sb("eps_t", [EMB, 2])
        fabs = sb("fabs", [EMB, NEPS + 2 * EMB])
        froot = sb("froot", [EMB, NEPS + 2 * EMB])
        fsign = sb("fsign", [EMB, NEPS + 2 * EMB])
        fnoise = sb("fnoise", [EMB, NEPS + 2 * EMB])
        sig_eo = sb("sig_eo", [EMB, 2, K_IN, EMB])
        wn = sb("wn", [EMB, 2, K_IN, EMB])
        bn = sb("bn", [EMB, 2])
        g_s = sb("g_s", [EMB, HALVES, HP])
        gcap = sb("gcap", [EMB, HALVES, HP])
        eg = sb("eg", [EMB, HALVES, HP])
        tnum = sb("tnum", [EMB, HALVES, HP])
        tden = sb("tden", [EMB, HALVES, HP])
        trec = sb("trec", [EMB, HALVES, HP])
        gnum = sb("gnum", [EMB, HALVES, HP])
        inum = sb("inum", [EMB, HALVES, HP])
        prod = sb("prod", [EMB, HALVES, HP])
        X = sb("X", [EMB, HALVES, HI, TOKENS])
        XB = sb("XB", [EMB, HALVES, HT])
        sq = sb("sq", [EMB, 3, HALVES, HT])
        lnv = sb("lnv", [EMB, 3, HALVES, HT])
        rstd = sb("rstd", [EMB, 3, HALVES, HT])
        n1 = sb("n1", [EMB, HALVES, HT])
        qkv_f = sb("qkv_f", [EMB, HALVES, HI, 3, TOKENS])
        qkv_c = sb("qkv_c", [EMB, HALVES, CHUNKS, 3, TOKENS])
        qkv_l = sb("qkv_l", [EMB, HALVES, 3, TOKENS, CHUNKS])
        v1 = sb("v1", [TOKENS, HALVES, GROUPS, HI, DH + 1])
        mx = sb("mx", [TOKENS, 2, UNIT])
        prob = sb("prob", [TOKENS, 2, UNIT, TOKENS])
        probT = sb("probT", [TOKENS, 2, UNIT, TOKENS])
        rden = sb("rden", [TOKENS, 2, UNIT])
        ctxn = sb("ctxn", [TOKENS, HALVES, GROUPS, HI, 32])
        ctx_c = sb("ctx_c", [EMB, HALVES, CHUNKS, TOKENS])
        ctx_f = sb("ctx_f", [EMB, HALVES, HI, TOKENS])
        y = sb("y", [EMB, HALVES, HT])
        z = sb("z", [EMB, HALVES, HT])
        h2 = sb("h2", [EMB, HALVES, HT])
        zf = sb("zf", [EMB, HALVES, HT])
        flat = sb("flat", [EMB, HALVES, HT])
        ea = sb("ea", [EMB, 2, HT])
        da = sb("da", [EMB, 2, HT])
        ra = sb("ra", [EMB, 2, HT])
        sa = sb("sa", [EMB, 2, HT])
        hid = sb("hid", [EMB, HALVES, PAIRS, HT])
        cb_s = sb("cb_s", [EMB, 2, HT])
        hsc = sb("hsc", [EMB, 3, NK, HT])
        hsp = sb("hsp", [EMB, 2, NK, HT])
        o_s = sb("o_s", [EMB, HALVES, HT])
        lg = sb("lg", [TOKENS, HALVES, HI, NG])
        gm = sb("gm", [TOKENS, HALVES, HI, EGROUPS])
        em = sb("em", [TOKENS, HALVES, HI, EGROUPS, EG])
        es = sb("es", [TOKENS, HALVES, HI, EG])
        emax = sb("emax", [TOKENS, HALVES, HI])
        ed = sb("ed", [TOKENS, HALVES, HI, EG])
        ee = sb("ee", [TOKENS, HALVES, HI, EG])
        esum = sb("esum", [TOKENS, HALVES, HI])
        erec = sb("erec", [TOKENS, HALVES, HI])
        pr = sb("pr", [TOKENS, HALVES, HI, EG])
        gt = sb("gt", [TOKENS, HALVES, HI, EG * EG])
        eq = sb("eq", [TOKENS, HALVES, HI, EG * EG])
        rank = sb("rank", [TOKENS, HALVES, HI, EG])
        top = sb("top", [TOKENS, HALVES, HI, EG])
        ptop = sb("ptop", [TOKENS, HALVES, HI, EG])
        psum_top = sb("psum_top", [TOKENS, HALVES, HI])
        rtop = sb("rtop", [TOKENS, HALVES, HI])
        wtop = sb("wtop", [TOKENS, HALVES, HI, EG])
        comb = sb("comb", [TOKENS, HALVES, HI, EXPERTS])
        rest = sb("rest", [TOKENS, HALVES, HI, EXPERTS])
        route = sb("route", [TOKENS, HALVES, HI, 4, EXPERTS], BF16)
        identb = sb("identb", [EMB, EMB], BF16)
        routeT = sb("routeT", [32, HALVES, HT], BF16)
        routeTf = sb("routeTf", [32, HALVES, HT])

        PS = ctx.enter_context(nc.psum_tensor("PS", [EMB, 8, BANK], F32))
        pf = PS[:].rearrange("p b n -> p (b n)")

        def bank(b, n=BANK, rows=EMB):
            return PS[0:rows, b, 0:n]

        s_cols, s_eob, s_wtok, s_x = sem("s_cols"), sem("s_eob"), sem("s_wtok"), [sem("s_x0"), sem("s_x1")]
        s_w3pe, s_stats, s_wqkvo, s_win = sem("s_w3pe"), sem("s_stats"), sem("s_wqkvo"), sem("s_win")
        s_wso, s_weo, s_gates = sem("s_wso"), sem("s_weo"), sem("s_gates")
        s_zero, s_ones, s_zctx, s_selb, s_identb, s_eps = (sem("s_zero"), sem("s_ones"), sem("s_zctx"), sem("s_selb"),
                                                           sem("s_identb"), sem("s_eps"))
        s_fabs, s_froot, s_fsign, s_fnoise = sem("s_fabs"), sem("s_froot"), sem("s_fsign"), sem("s_fnoise")
        s_sig, s_wn, s_bn = sem("s_sig"), sem("s_wn"), sem("s_bn")
        s_gate_mm, s_inner_mm, s_g, s_gcap, s_eg = sem("s_gate_mm"), sem("s_inner_mm"), sem("s_g"), sem("s_gcap"), sem("s_eg")
        s_emb = sem("s_emb")
        s_prod, s_tok_mm, s_X, s_cls, s_XB = sem("s_prod"), sem("s_tok_mm"), sem("s_X"), sem("s_cls"), sem("s_XB")
        s_cen = [sem(f"s_cen{i}") for i in range(3)]
        s_sq = [sem(f"s_sq{i}") for i in range(3)]
        s_var = [sem(f"s_var{i}") for i in range(3)]
        s_lnv = [sem(f"s_lnv{i}") for i in range(3)]
        s_rstd = [sem(f"s_rstd{i}") for i in range(3)]
        s_n1 = sem("s_n1")
        s_qkv_mm, s_qk, s_v, s_qkvc = sem("s_qkv_mm"), sem("s_qk"), sem("s_v"), [sem("s_qkvc0"), sem("s_qkvc1")]
        s_lq, s_lk, s_lv, s_vT, s_v1 = sem("s_lq"), sem("s_lk"), sem("s_lv"), sem("s_vT"), sem("s_v1")
        s_score, s_mx, s_sub, s_exp, s_pT, s_pTs, s_pv, s_rden, s_ctxn = (
            sem("s_score"), sem("s_mx"), sem("s_sub"), sem("s_exp"), sem("s_pT"), sem("s_pTs"), sem("s_pv"),
            sem("s_rden"), sem("s_ctxn"))
        s_ctxT, s_ctxc, s_ctxf = sem("s_ctxT"), sem("s_ctxc"), [sem("s_ctxf0"), sem("s_ctxf1")]
        s_o_mm, s_y, s_z, s_h2, s_zf, s_flat = sem("s_o_mm"), sem("s_y"), sem("s_z"), sem("s_h2"), sem("s_zf"), sem("s_flat")
        s_lg_mm, s_route_step, s_ed, s_ee, s_route, s_routeT_mm, s_routeT, s_routeTf = (
            sem("s_lg_mm"), sem("s_route_step"), sem("s_ed"), sem("s_ee"), sem("s_route"), sem("s_routeT_mm"),
            sem("s_routeT"), sem("s_routeTf"))
        s_ab, s_ea, s_da, s_ra, s_sa, s_hid = sem("s_ab"), sem("s_ea"), sem("s_da"), sem("s_ra"), sem("s_sa"), sem("s_hid")
        s_cb, s_cbs, s_hsc, s_hsp, s_ehid, s_ymm = sem("s_cb"), sem("s_cbs"), sem("s_hsc"), sem("s_hsp"), sem("s_ehid"), sem("s_ymm")
        s_o, s_out = sem("s_o"), sem("s_out")

        def score(gq, b):
            return PS[0:TOKENS, b, 0:4 * TOKENS].rearrange("p (g k) -> p g k", k=TOKENS)

        scores = PS[0:TOKENS, 0:2, 0:4 * TOKENS].rearrange("p b (g k) -> p b g k", k=TOKENS)
        probTs = PS[0:TOKENS, 2:4, 0:4 * TOKENS].rearrange("p b (g k) -> p b g k", k=TOKENS)
        pv = PS[0:TOKENS, 4, 0:UNIT * 32].rearrange("p (g d) -> p g d", d=32)
        vT = PS[0:TOKENS, 6:8, :].rearrange("p b (g c) -> p (b g) c", c=EMB)
        ctxT = pf[:, 6 * BANK + CT0:6 * BANK + CT0 + CHUNKS * TOKENS]

        def pair_banks(n):
            return (2 * (n % 3), 2 * (n % 3) + 1)

        def y_bank(h):
            return 6 + h

        def routeT_p(h):
            return PS[0:32, y_bank(h), 0:HI * 33].bitcast(BF16).rearrange("p (i t) -> p i t", i=HI)[:, :, 0:TOKENS]

        def logits(h):
            return PS[0:TOKENS, y_bank(h), 0:HI * 16].rearrange("p (i n) -> p i n", i=HI)[:, :, 0:NG]

        def dve_experts(h, e):
            per = EXPERTS - len(POOL_EXPERTS)
            return h * per + len([i for i in range(e + 1) if i not in POOL_EXPERTS])

        def pool_experts(h, e):
            return h * len(POOL_EXPERTS) + len([i for i in range(e + 1) if i in POOL_EXPERTS])

        block = ctx.enter_context(nc.Block())

        @block.sync
        def _(sp):
            sp.dma_start(eps_in[:, NEPS:NEPS + 2 * EMB], eob.partition_broadcast(EMB)).then_inc(s_eob, 16)
            sp.dma_start(x_s[:, 0], patches[0]).then_inc(s_x[0], 16)
            sp.dma_start(x_s[:, 1], patches[1]).then_inc(s_x[1], 16)
            sp.dma_start(w3pe_s[:], w3pe).then_inc(s_w3pe, 16)
            sp.dma_start(wqkvo_s[:], wqkvo).then_inc(s_wqkvo, 16)
            sp.dma_start(win_s[:], win).then_inc(s_win, 16)
            sp.dma_start(weo_s[:], weo).then_inc(s_weo, 16)
            for h in range(HALVES):
                sp.wait_ge(s_qk, 2 * (h + 1))
                sp.wait_ge(s_v, h + 1)
                sp.wait_ge(s_zero, 1)
                for i in range(HI):
                    sp.dma_start(qkv_c[32 * i:32 * i + DH, h].rearrange("d j c t -> d j (c t)"),
                                 qkv_f[:, h, i].rearrange("p c t -> p (c t)")).then_inc(s_qkvc[h], 16)
            for h in range(HALVES):
                sp.wait_ge(s_ctxc, h + 1)
                for i in range(HI):
                    sp.dma_start(ctx_f[:, h, i, :], ctx_c[32 * i:32 * i + DH, h]).then_inc(s_ctxf[h], 16)
            for h in range(HALVES):
                sp.wait_ge(s_o, h + 1)
                sp.dma_start(out[:, h * HT:(h + 1) * HT], o_s[:, h]).then_inc(s_out, 16)
            sp.wait_ge(s_out, 16 * HALVES)

        @block.gpsimd
        def _(pool):
            nc.gpsimd.memset(qkv_c[:], 0.0).then_inc(s_zero, 1)
            nc.gpsimd.memset(v1[:], 1.0).then_inc(s_ones, 1)
            nc.gpsimd.memset(ctxn[:], 0.0).then_inc(s_zctx, 1)
            pool.wait_ge(s_gates, 16 * 4)
            nc.gpsimd.tensor_copy(selb[:], sel_s[:]).then_inc(s_selb, 1)
            pool.wait_ge(s_stats, 16)
            nc.gpsimd.tensor_copy(identb[:], ident).then_inc(s_identb, 1)
            for h in range(HALVES):
                pool.wait_ge(s_X, h + 1)
                pool.wait_ge(s_cls, 1)
                nc.gpsimd.tensor_scalar(XB[:, h], X[:, h].rearrange("p i t -> p (i t)"),
                                        cols_s[:, C_BETA:C_BETA + 1], None, ALU.add).then_inc(s_XB, 1)
            for h in range(HALVES):
                pool.wait_ge(s_qkvc[h], 16 * HI)
                nc.gpsimd.tensor_copy(qkv_l[:, h, 2].rearrange("p t j -> p j t"), qkv_c[:, h, :, 2]).then_inc(s_lv, 1)
            for h in range(HALVES):
                for q in range(PAIRS):
                    n = h * PAIRS + q
                    pool.wait_ge(s_ea, n + 1)
                    if n >= 2:
                        pool.wait_ge(s_ra, n - 1)
                    nc.gpsimd.tensor_scalar(da[:, n % 2], ea[:, n % 2], 1.0, None, ALU.add).then_inc(s_da, 1)
                for e in POOL_EXPERTS:
                    n = pool_experts(h, e)
                    pool.wait_ge(s_cbs, n)
                    pool.wait_ge(s_hid, (h + 1) * PAIRS)
                    if n > 2:
                        pool.wait_ge(s_ehid, h * EXPERTS + e - 2)
                    nc.gpsimd.tensor_tensor(hsp[:, n % 2], hid[:, h, NK:PAIRS],
                                            cb_s[:, n % 2].unsqueeze(1).to_broadcast([EMB, NK, HT]),
                                            ALU.mult).then_inc(s_hsp, 1)

        @block.scalar
        def _(act):
            act.dma_start(cols_s[:], cols).then_inc(s_cols, 16)
            act.dma_start(eps_in[:, 0:NEPS], cols[:, 0:NEPS]).then_inc(s_cols, 16)
            act.dma_start(wtok_s[:], wtok).then_inc(s_wtok, 16)
            act.dma_start(stats_s[:], stats).then_inc(s_stats, 16)
            act.dma_start(gates_s[:], gates).then_inc(s_gates, 16)
            act.dma_start(gbias_s[:], gbias).then_inc(s_gates, 16)
            act.dma_start(ebias_s[:], ebias).then_inc(s_gates, 16)
            act.dma_start(sel_s[:], sel).then_inc(s_gates, 16)
            act.dma_start(wso_s[:], wso).then_inc(s_wso, 16)
            act.wait_ge(s_cols, 32)
            act.wait_ge(s_eob, 16)
            nc.scalar.activation(fabs[:], eps_in[:], ACT.Abs).then_inc(s_fabs, 1)
            nc.scalar.activation(fsign[:], eps_in[:], ACT.Sign).then_inc(s_fsign, 1)
            act.wait_ge(s_fabs, 1)
            nc.scalar.activation(froot[:], fabs[:], ACT.Sqrt).then_inc(s_froot, 1)
            nc.scalar.preload_act_table_set("natural_log_exp_and_others")
            act.wait_ge(s_bn, 2)
            for h in range(HALVES):
                act.wait_ge(s_gate_mm, h + 1)
                nc.scalar.activation(g_s[:, h], bank(2 * h, HP), ACT.Identity, bias=bn[:, 0:1]).then_inc(s_g, 1)
            for h in range(HALVES):
                act.wait_ge(s_gcap, h + 1)
                nc.scalar.activation(eg[:, h], gcap[:, h], ACT.Exp).then_inc(s_eg, 1)

            def norm_square(use, h, cen_bank):
                act.wait_ge(s_cen[use], h + 1)
                nc.scalar.activation(sq[:, use, h], bank(cen_bank, HT), ACT.Square).then_inc(s_sq[use], 1)

            def norm_rstd(use, h, var_bank, scale=1.0):
                act.wait_ge(s_var[use], h + 1)
                nc.scalar.activation(lnv[:, use, h], bank(var_bank, HT), ACT.Ln, scale=scale,
                                     bias=eps_t[:, int(use == 2):int(use == 2) + 1]).then_inc(s_lnv[use], 1)
                act.wait_ge(s_lnv[use], h + 1)
                nc.scalar.activation(rstd[:, use, h], lnv[:, use, h], ACT.Exp, scale=-0.5).then_inc(s_rstd[use], 1)

            act.wait_ge(s_eps, 2)
            for h in range(HALVES):
                norm_square(0, h, 6 + h)
            for h in range(HALVES):
                norm_rstd(0, h, h)
            for h in range(HALVES):
                act.wait_ge(s_qkv_mm, 3 * h + 1)
                nc.scalar.activation(qkv_f[:, h, :, 0], bank((2, 5)[h], HT).rearrange("p (i t) -> p i t", i=HI), ACT.Identity,
                                     bias=cols_s[:, C_BQ:C_BQ + 1]).then_inc(s_qk, 1)
                act.wait_ge(s_qkv_mm, 3 * h + 2)
                nc.scalar.activation(qkv_f[:, h, :, 1], bank((3, 0)[h], HT).rearrange("p (i t) -> p i t", i=HI), ACT.Identity,
                                     bias=cols_s[:, C_BK:C_BK + 1]).then_inc(s_qk, 1)

            def keys_values(h):
                act.wait_ge(s_qkvc[h], 16 * HI)
                nc.scalar.copy(qkv_l[:, h, 1].rearrange("p t j -> p j t"), qkv_c[:, h, :, 1]).then_inc(s_lk, 1)
                act.wait_ge(s_vT, h + 1)
                act.wait_ge(s_ones, 1)
                nc.scalar.copy(v1[:, h, :, :, 0:DH],
                               vT.rearrange("p g (i d) -> p g i d", d=32)[:, :, :, 0:DH]).then_inc(s_v1, 1)

            def context_out(h):
                act.wait_ge(s_ctxT, h + 1)
                nc.scalar.copy(ctx_c[:, h].rearrange("p j t -> p t j"),
                               ctxT.rearrange("p (t j) -> p t j", j=CHUNKS)).then_inc(s_ctxc, 1)

            keys_values(0)
            for n in range(HALVES * UNITS):
                act.wait_ge(s_sub, n + 1)
                nc.scalar.activation(prob[:, n % 2], prob[:, n % 2], ACT.Exp, scale=SCALE).then_inc(s_exp, 1)
                act.wait_ge(s_pT, n + 1)
                if n >= 2:
                    act.wait_ge(s_pv, n - 1)
                nc.scalar.copy(probT[:, n % 2].rearrange("p (b g) k -> p b g k", b=2), probTs).then_inc(s_pTs, 1)
                if n == AHEAD:
                    keys_values(1)
                if n == UNITS:
                    context_out(0)
            context_out(1)
            for h in range(HALVES):
                norm_square(1, h, 4 * h + 1)
            for h in range(HALVES):
                norm_rstd(1, h, 4 * h + 2)
            for h in range(HALVES):
                norm_square(2, h, 4 * h + 3)
            for h in range(HALVES):
                norm_rstd(2, h, 4 * h, 1.0 + EPS)
            for h in range(HALVES):
                for q in range(PAIRS):
                    n = h * PAIRS + q
                    act.wait_ge(s_ab, n + 1)
                    if n >= 2:
                        act.wait_ge(s_da, n - 1)
                    nc.scalar.activation(ea[:, n % 2], bank(pair_banks(n)[0], HT), ACT.Exp, scale=-1.0).then_inc(s_ea, 1)
                    if q == 0:
                        act.wait_ge(s_ed, h + 1)
                        nc.scalar.activation(ee[:, h], ed[:, h], ACT.Exp).then_inc(s_ee, 1)
                act.wait_ge(s_routeT_mm, h + 1)
                nc.scalar.copy(routeT[:, h].rearrange("p (i t) -> p i t", i=HI), routeT_p(h)).then_inc(s_routeT, 1)
                nc.scalar.copy(routeTf[:, h].rearrange("p (i t) -> p i t", i=HI), routeT_p(h)).then_inc(s_routeTf, 1)
                for e in POOL_EXPERTS:
                    n = pool_experts(h, e)
                    act.wait_ge(s_cb, h * EXPERTS + e + 1)
                    if n > 2:
                        act.wait_ge(s_hsp, n - 2)
                    nc.scalar.copy(cb_s[:, n % 2], bank(e % 6, HT)).then_inc(s_cbs, 1)

        @block.vector
        def _(dve):
            step = [0]

            def routed(ins):
                step[0] += 1
                ins.then_inc(s_route_step, 1)
                dve.wait_ge(s_route_step, step[0])

            nc.vector.memset(eps_t[:, 0:1], EPS).then_inc(s_eps, 1)
            nc.vector.memset(eps_t[:, 1:2], EPS * EPS).then_inc(s_eps, 1)
            dve.wait_ge(s_cols, 32)
            nc.vector.tensor_copy(X[:, :, :, 0:1], cols_s[:, C_CLS:C_CLS + 1].unsqueeze(1).unsqueeze(1)
                                  .to_broadcast([EMB, HALVES, HI, 1])).then_inc(s_cls, 1)
            dve.wait_ge(s_froot, 1)
            dve.wait_ge(s_fsign, 1)
            nc.vector.tensor_tensor(fnoise[:], froot[:], fsign[:], ALU.mult).then_inc(s_fnoise, 1)
            dve.wait_ge(s_fnoise, 1)
            dve.wait_ge(s_wtok, 16)
            for net in range(2):
                nc.vector.tensor_tensor(sig_eo[:, net], wtok_s[:, net, 1],
                                        fnoise[:, NEPS + net * EMB:NEPS + (net + 1) * EMB].unsqueeze(1)
                                        .to_broadcast([EMB, K_IN, EMB]), ALU.mult).then_inc(s_sig, 1)
                dve.wait_ge(s_sig, net + 1)
                for k in range(K_IN):
                    c = 2 * net + k
                    nc.vector.scalar_tensor_tensor(out=wn[:, net, k], in0=sig_eo[:, net, k],
                                                   scalar=fnoise[:, c:c + 1], in1=wtok_s[:, net, 0, k],
                                                   op0=ALU.mult, op1=ALU.add).then_inc(s_wn, 1)
            for net in range(2):
                nc.vector.scalar_tensor_tensor(out=bn[:, net:net + 1], in0=cols_s[:, C_SB1 + net:C_SB1 + net + 1],
                                               scalar=fnoise[:, C_EO1 + net:C_EO1 + net + 1],
                                               in1=cols_s[:, C_B1 + net:C_B1 + net + 1],
                                               op0=ALU.mult, op1=ALU.add).then_inc(s_bn, 1)
            for h in range(HALVES):
                dve.wait_ge(s_g, h + 1)
                nc.vector.tensor_scalar_min(gcap[:, h], g_s[:, h], GATE_CAP).then_inc(s_gcap, 1)
            c = 0
            for h in range(HALVES):
                dve.wait_ge(s_eg, h + 1)
                nc.vector.scalar_tensor_tensor(out=tnum[:, h], in0=eg[:, h], scalar=2.0, in1=eg[:, h],
                                               op0=ALU.add, op1=ALU.mult).then_inc(s_emb, 1)
                dve.wait_ge(s_emb, c + 1)
                nc.vector.tensor_scalar_add(tden[:, h], tnum[:, h], 2.0).then_inc(s_emb, 1)
                nc.vector.tensor_tensor(gnum[:, h], g_s[:, h], tnum[:, h], ALU.mult).then_inc(s_emb, 1)
                dve.wait_ge(s_emb, c + 2)
                nc.vector.reciprocal(trec[:, h], tden[:, h]).then_inc(s_emb, 1)
                dve.wait_ge(s_inner_mm, h + 1)
                dve.wait_ge(s_bn, 2)
                dve.wait_ge(s_emb, c + 3)
                nc.vector.scalar_tensor_tensor(out=inum[:, h], in0=bank(2 * h + 1, HP), scalar=bn[:, 1:2],
                                               in1=gnum[:, h], op0=ALU.add, op1=ALU.mult).then_inc(s_emb, 1)
                dve.wait_ge(s_emb, c + 5)
                nc.vector.tensor_tensor(prod[:, h], inum[:, h], trec[:, h], ALU.mult).then_inc(s_prod, 1)
                c += 5
            dve.wait_ge(s_w3pe, 16)
            for h in range(HALVES):
                dve.wait_ge(s_tok_mm, h + 1)
                nc.vector.scalar_tensor_tensor(
                    out=X[:, h, :, 1:TOKENS], in0=bank(4 + h, HP).rearrange("p (i t) -> p i t", i=HI),
                    scalar=cols_s[:, C_B3:C_B3 + 1],
                    in1=w3pe_s[:, EMB:EMB + PATCHES].unsqueeze(1).to_broadcast([EMB, HI, PATCHES]),
                    op0=ALU.add, op1=ALU.add).then_inc(s_X, 1)
            for h in range(HALVES):
                dve.wait_ge(s_rstd[0], h + 1)
                nc.vector.tensor_tensor(n1[:, h], bank(6 + h, HT), rstd[:, 0, h], ALU.mult).then_inc(s_n1, 1)
            for h in range(HALVES):
                dve.wait_ge(s_qkv_mm, 3 * h + 3)
                nc.vector.tensor_scalar(qkv_f[:, h, :, 2], bank((4, 1)[h], HT).rearrange("p (i t) -> p i t", i=HI),
                                        cols_s[:, C_BV:C_BV + 1], None, ALU.add).then_inc(s_v, 1)
            for h in range(HALVES):
                dve.wait_ge(s_qkvc[h], 16 * HI)
                nc.vector.tensor_copy(qkv_l[:, h, 0].rearrange("p t j -> p j t"), qkv_c[:, h, :, 0]).then_inc(s_lq, 1)

            def softmax_shift(n):
                dve.wait_ge(s_score, n + 1)
                nc.vector.tensor_reduce(mx[:, n % 2].rearrange("p (b g) -> p b g", b=2), scores, AX.X,
                                        ALU.max).then_inc(s_mx, 1)
                dve.wait_ge(s_mx, n + 1)
                if n >= 2:
                    dve.wait_ge(s_pT, n - 1)
                nc.vector.tensor_tensor(prob[:, n % 2].rearrange("p (b g) k -> p b g k", b=2), scores,
                                        mx[:, n % 2].rearrange("p (b g) -> p b g", b=2).unsqueeze(3)
                                        .to_broadcast([TOKENS, 2, 4, TOKENS]), ALU.subtract).then_inc(s_sub, 1)

            def context_norm(n):
                h, u = n // UNITS, n % UNITS
                ip, gq = u // 2, u % 2
                dve.wait_ge(s_pv, n + 1)
                nc.vector.reciprocal(rden[:, n % 2], pv[:, :, DH]).then_inc(s_rden, 1)
                dve.wait_ge(s_rden, n + 1)
                nc.vector.tensor_tensor(
                    ctxn[:, h, 4 * gq:4 * gq + 4, 2 * ip:2 * ip + 2, 0:DH].rearrange("p g b d -> p b g d"),
                    pv[:, :, 0:DH].rearrange("p (b g) d -> p b g d", b=2),
                    rden[:, n % 2].rearrange("p (b g) -> p b g", b=2).unsqueeze(3)
                    .to_broadcast([TOKENS, 2, 4, DH]), ALU.mult).then_inc(s_ctxn, 1)

            dve.wait_ge(s_zctx, 1)
            softmax_shift(0)
            for n in range(HALVES * UNITS):
                if n + 1 < HALVES * UNITS:
                    softmax_shift(n + 1)
                context_norm(n)

            for h in range(HALVES):
                dve.wait_ge(s_o_mm, h + 1)
                nc.vector.scalar_tensor_tensor(out=y[:, h], in0=bank(4 * h, HT), scalar=cols_s[:, C_BO:C_BO + 1],
                                               in1=n1[:, h], op0=ALU.add, op1=ALU.add).then_inc(s_y, 1)
            for h in range(HALVES):
                dve.wait_ge(s_rstd[1], h + 1)
                nc.vector.tensor_tensor(z[:, h], bank(4 * h + 1, HT), rstd[:, 1, h], ALU.mult).then_inc(s_z, 1)
                dve.wait_ge(s_z, h + 1)
                dve.wait_ge(s_XB, h + 1)
                nc.vector.scalar_tensor_tensor(out=h2[:, h], in0=z[:, h], scalar=cols_s[:, C_GAMMA:C_GAMMA + 1],
                                               in1=XB[:, h], op0=ALU.mult, op1=ALU.add).then_inc(s_h2, 1)
            for h in range(HALVES):
                dve.wait_ge(s_rstd[2], h + 1)
                nc.vector.tensor_tensor(zf[:, h], bank(4 * h + 3, HT), rstd[:, 2, h], ALU.mult).then_inc(s_zf, 1)
                dve.wait_ge(s_zf, h + 1)
                nc.vector.tensor_scalar(flat[:, h], zf[:, h], cols_s[:, C_LNS:C_LNS + 1],
                                        cols_s[:, C_LNB:C_LNB + 1], ALU.mult, ALU.add).then_inc(s_flat, 1)

            def router(h):
                dve.wait_ge(s_lg_mm, h + 1)
                routed(nc.vector.tensor_tensor(
                    lg[:, h], logits(h),
                    gbias_s[:, 0:NG].unsqueeze(1).to_broadcast([TOKENS, HI, NG]), ALU.add))
                nc.vector.tensor_tensor(gm[:, h, :, 0:1], lg[:, h, :, 0:1], lg[:, h, :, 1:2], ALU.is_ge)
                step[0] += 0
                routed(nc.vector.tensor_tensor(gm[:, h, :, 1:2], lg[:, h, :, 0:1], lg[:, h, :, 1:2], ALU.is_lt))
                gmb = gm[:, h].unsqueeze(3).to_broadcast([TOKENS, HI, EGROUPS, EG])
                routed(nc.vector.tensor_tensor(em[:, h], lg[:, h, :, EGROUPS:NG].rearrange("p i (g e) -> p i g e", e=EG),
                                               gmb, ALU.mult))
                routed(nc.vector.tensor_tensor(es[:, h], em[:, h, :, 0], em[:, h, :, 1], ALU.add))
                routed(nc.vector.tensor_reduce(emax[:, h], es[:, h], AX.X, ALU.max))

                def per_image(t):
                    return t[:, h].unsqueeze(2).to_broadcast([TOKENS, HI, EG])

                nc.vector.tensor_tensor(ed[:, h], es[:, h], per_image(emax), ALU.subtract).then_inc(s_ed, 1)
                dve.wait_ge(s_ee, h + 1)
                routed(nc.vector.tensor_reduce(esum[:, h], ee[:, h], AX.X, ALU.add))
                routed(nc.vector.reciprocal(erec[:, h], esum[:, h]))
                routed(nc.vector.tensor_tensor(pr[:, h], ee[:, h], per_image(erec), ALU.mult))
                p_j = pr[:, h].unsqueeze(2).to_broadcast([TOKENS, HI, EG, EG])
                p_e = pr[:, h].unsqueeze(3).to_broadcast([TOKENS, HI, EG, EG])
                sq4 = "p i (e j) -> p i e j"
                nc.vector.tensor_tensor(gt[:, h].rearrange(sq4, e=EG), p_j, p_e, ALU.is_gt)
                routed(nc.vector.tensor_tensor(eq[:, h].rearrange(sq4, e=EG), p_j, p_e, ALU.is_equal))
                routed(nc.vector.tensor_tensor(eq[:, h], eq[:, h],
                                               gbias_s[:, NG:NG + EG * EG].unsqueeze(1)
                                               .to_broadcast([TOKENS, HI, EG * EG]), ALU.mult))
                routed(nc.vector.tensor_tensor(gt[:, h], gt[:, h], eq[:, h], ALU.add))
                routed(nc.vector.tensor_reduce(rank[:, h], gt[:, h].rearrange(sq4, e=EG), AX.X, ALU.add))
                routed(nc.vector.tensor_single_scalar(top[:, h], rank[:, h], 1.5, ALU.is_lt))
                routed(nc.vector.tensor_tensor(ptop[:, h], pr[:, h], top[:, h], ALU.mult))
                routed(nc.vector.tensor_reduce(psum_top[:, h], ptop[:, h], AX.X, ALU.add))
                routed(nc.vector.tensor_scalar_add(psum_top[:, h], psum_top[:, h], TOPK_EPS))
                routed(nc.vector.reciprocal(rtop[:, h], psum_top[:, h]))
                routed(nc.vector.tensor_tensor(wtop[:, h], ptop[:, h], per_image(rtop), ALU.mult))
                ge = "p i (g e) -> p i g e"

                def both_groups(t):
                    return t[:, h].unsqueeze(2).to_broadcast([TOKENS, HI, EGROUPS, EG])

                routed(nc.vector.tensor_tensor(comb[:, h].rearrange(ge, e=EG), both_groups(wtop), gmb, ALU.mult))
                routed(nc.vector.tensor_copy(route[:, h, :, 0], comb[:, h]))
                routed(nc.vector.tensor_tensor(rest[:, h], comb[:, h], route[:, h, :, 0], ALU.subtract))
                routed(nc.vector.tensor_copy(route[:, h, :, 1], rest[:, h]))
                nc.vector.tensor_tensor(route[:, h, :, 2], rest[:, h], route[:, h, :, 1], ALU.subtract).then_inc(s_route, 1)
                nc.vector.tensor_tensor(route[:, h, :, 3].rearrange(ge, e=EG), both_groups(top), gmb,
                                        ALU.mult).then_inc(s_route, 1)

            def swiglu(n):
                h, q = n // PAIRS, n % PAIRS
                a, b = (bank(x, HT) for x in pair_banks(n))
                dve.wait_ge(s_da, n + 1)
                nc.vector.reciprocal(ra[:, n % 2], da[:, n % 2]).then_inc(s_ra, 1)
                dve.wait_ge(s_ra, n + 1)
                nc.vector.tensor_tensor(sa[:, n % 2], a, ra[:, n % 2], ALU.mult).then_inc(s_sa, 1)
                dve.wait_ge(s_sa, n + 1)
                nc.vector.tensor_tensor(hid[:, h, q], b, sa[:, n % 2], ALU.mult).then_inc(s_hid, 1)

            for h in range(HALVES):
                router(h)
                for q in range(PAIRS):
                    swiglu(h * PAIRS + q)
                for e in range(EXPERTS):
                    if e in POOL_EXPERTS:
                        continue
                    n = dve_experts(h, e)
                    dve.wait_ge(s_cb, h * EXPERTS + e + 1)
                    dve.wait_ge(s_hid, (h + 1) * PAIRS)
                    if n > 3:
                        back = [(hh, i) for hh in range(HALVES) for i in range(EXPERTS) if i not in POOL_EXPERTS][n - 4]
                        dve.wait_ge(s_ehid, back[0] * EXPERTS + back[1] + 1)
                    nc.vector.tensor_tensor(hsc[:, n % 3], hid[:, h, NK:PAIRS],
                                            bank(e % 6, HT).unsqueeze(1).to_broadcast([EMB, NK, HT]),
                                            ALU.mult).then_inc(s_hsc, 1)
                dve.wait_ge(s_ymm, h + 1)
                nc.vector.scalar_tensor_tensor(out=o_s[:, h], in0=bank(y_bank(h), HT), scalar=cols_s[:, C_SOB:C_SOB + 1],
                                               in1=h2[:, h], op0=ALU.add, op1=ALU.add).then_inc(s_o, 1)

        @block.tensor
        def _(pe):
            mm = nc.tensor.matmul
            pe.wait_ge(s_wn, 4)
            for h in range(HALVES):
                pe.wait_ge(s_x[h], 16)
                for net, done in ((0, s_gate_mm), (1, s_inner_mm)):
                    for k in range(K_IN):
                        last = mm(bank(2 * h + net, HP), wn[:, net, k], x_s[:, h, k], start=(k == 0), stop=(k == K_IN - 1))
                    last.then_inc(done, 1)
            pe.wait_ge(s_w3pe, 16)
            for h in range(HALVES):
                pe.wait_ge(s_prod, h + 1)
                mm(bank(4 + h, HP), w3pe_s[:, 0:EMB], prod[:, h], start=True, stop=True).then_inc(s_tok_mm, 1)

            def norm_center(use, h, cen_bank, rows):
                mm(bank(cen_bank, HT), center, rows, start=True, stop=True).then_inc(s_cen[use], 1)

            def norm_var(use, h, var_bank):
                pe.wait_ge(s_sq[use], h + 1)
                mm(bank(var_bank, HT), mean, sq[:, use, h], start=True, stop=True).then_inc(s_var[use], 1)

            pe.wait_ge(s_stats, 16)
            pe.wait_ge(s_cls, 1)
            for h in range(HALVES):
                pe.wait_ge(s_X, h + 1)
                norm_center(0, h, 6 + h, X[:, h].rearrange("p i t -> p (i t)"))
            for h in range(HALVES):
                norm_var(0, h, h)
            pe.wait_ge(s_wqkvo, 16)
            for h in range(HALVES):
                pe.wait_ge(s_n1, h + 1)
                if h == 1:
                    pe.wait_ge(s_rstd[0], 2)
                for c in range(3):
                    mm(bank(((2, 3, 4), (5, 0, 1))[h][c], HT), wqkvo_s[:, c], n1[:, h], start=True,
                       stop=True).then_inc(s_qkv_mm, 1)

            def unit_place(n):
                h, u = n // UNITS, n % UNITS
                return h, 2 * (u // 2), 4 * (u % 2)

            def unit_scores(n):
                h, i0, g0 = unit_place(n)
                if n >= 1:
                    pe.wait_ge(s_sub, n)
                if n % UNITS == 0:
                    pe.wait_ge(s_lq, h + 1)
                    pe.wait_ge(s_lk, h + 1)
                q_l = qkv_l[:, h, 0].rearrange("p t j -> p (t j)")
                k_l = qkv_l[:, h, 1].rearrange("p t j -> p (t j)")
                for g in range(4):
                    for b in range(2):
                        rows = slice(32 * (i0 + b), 32 * (i0 + b) + DH)
                        keys = slice((g0 + g) * TOKENS, (g0 + g + 1) * TOKENS)
                        last = mm(score(0, b)[:, g], q_l[rows, keys], k_l[rows, keys], start=True, stop=True)
                last.then_inc(s_score, 1)

            def unit_transposes(n):
                pe.wait_ge(s_exp, n + 1)
                if n >= 1:
                    pe.wait_ge(s_pTs, n)
                for g in range(UNIT):
                    last = nc.tensor.transpose(probTs[:, g // 4, g % 4], prob[:, n % 2, g], ident[0:TOKENS, 0:TOKENS])
                last.then_inc(s_pT, 1)

            def unit_context(n):
                h, i0, g0 = unit_place(n)
                pe.wait_ge(s_pTs, n + 1)
                if n % UNITS == 0:
                    pe.wait_ge(s_v1, h + 1)
                if n >= 1:
                    pe.wait_ge(s_ctxn, n)
                for g in range(UNIT):
                    last = mm(pv[:, g, 0:DH + 1], probT[:, n % 2, g], v1[:, h, g0 + g % 4, i0 + g // 4],
                              start=True, stop=True)
                last.then_inc(s_pv, 1)

            def values(h):
                pe.wait_ge(s_lv, h + 1)
                if h == 0:
                    pe.wait_ge(s_n1, 2)
                if h == 1:
                    pe.wait_ge(s_v1, 1)
                v_l = qkv_l[:, h, 2].rearrange("p t j -> p (t j)")
                for g in range(GROUPS):
                    last = nc.tensor.transpose(vT[:, g], v_l[:, g * TOKENS:(g + 1) * TOKENS], ident)
                last.then_inc(s_vT, 1)

            def context_images(h):
                pe.wait_ge(s_ctxn, (h + 1) * UNITS)
                if h == 0:
                    pe.wait_ge(s_v1, 2)
                if h == 1:
                    pe.wait_ge(s_ctxc, 1)
                for g in range(GROUPS):
                    last = nc.tensor.transpose(ctxT[:, g * TOKENS:(g + 1) * TOKENS],
                                               ctxn[:, h, g].rearrange("p i d -> p (i d)"), ident[0:TOKENS, 0:TOKENS])
                last.then_inc(s_ctxT, 1)

            pe.wait_ge(s_qk, 4)
            pe.wait_ge(s_v, 2)
            values(0)
            unit_scores(0)
            for n in range(HALVES * UNITS):
                if n == AHEAD:
                    values(1)
                if n + 1 < HALVES * UNITS:
                    unit_scores(n + 1)
                unit_transposes(n)
                unit_context(n)
                if n == UNITS:
                    context_images(0)
            context_images(1)

            pe.wait_ge(s_ctxc, 2)
            pe.wait_ge(s_ctxn, 2 * UNITS)
            for h in range(HALVES):
                pe.wait_ge(s_ctxf[h], 16 * HI)
                mm(bank(4 * h, HT), wqkvo_s[:, 3], ctx_f[:, h].rearrange("p i t -> p (i t)"), start=True,
                   stop=True).then_inc(s_o_mm, 1)
            for h in range(HALVES):
                pe.wait_ge(s_y, h + 1)
                norm_center(1, h, 4 * h + 1, y[:, h])
            for h in range(HALVES):
                norm_var(1, h, 4 * h + 2)
            for h in range(HALVES):
                pe.wait_ge(s_h2, h + 1)
                norm_center(2, h, 4 * h + 3, h2[:, h])
            for h in range(HALVES):
                norm_var(2, h, 4 * h)
            pe.wait_ge(s_gates, 16 * 4)
            for h in range(HALVES):
                pe.wait_ge(s_flat, h + 1)
                for i in range(HI):
                    last = mm(logits(h)[:, i], flat[:, h, i * TOKENS:(i + 1) * TOKENS],
                              gates_s[:], start=True, stop=True)
                last.then_inc(s_lg_mm, 1)
            pe.wait_ge(s_win, 16)
            pe.wait_ge(s_wso, 16)
            pe.wait_ge(s_weo, 16)
            pe.wait_ge(s_selb, 1)
            pe.wait_ge(s_identb, 1)
            pe.wait_ge(s_rstd[2], 2)
            for h in range(HALVES):
                for q in range(PAIRS):
                    n = h * PAIRS + q
                    if n == 0:
                        pe.wait_ge(s_zf, 2)
                    if h == 1:
                        pe.wait_ge(s_hsc, dve_experts(0, EXPERTS - 1))
                        pe.wait_ge(s_cbs, len(POOL_EXPERTS))
                    if q == 3 or n >= 3:
                        pe.wait_ge(s_hid, n - 2)
                    if n == 2:
                        pe.wait_ge(s_zf, 2)
                    for ab, b in zip(range(2), pair_banks(n)):
                        last = mm(bank(b, HT), win_s[:, q // NK, NK * ab + q % NK], flat[:, h], start=True, stop=True)
                    last.then_inc(s_ab, 1)
                pe.wait_ge(s_route, 2 * (h + 1))
                for i in range(HI):
                    last = nc.tensor.transpose(routeT_p(h)[:, i],
                                               route[:, h, i].rearrange("p a e -> p (a e)"), identb[0:TOKENS, 0:TOKENS])
                last.then_inc(s_routeT_mm, 1)
                pe.wait_ge(s_hid, (h + 1) * PAIRS)
                pe.wait_ge(s_routeTf, h + 1)
                for k in range(NK):
                    mm(bank(y_bank(h), HT), wso_s[:, k], hid[:, h, k], start=(k == 0), stop=False)

                def broadcast(e):
                    if e == 0:
                        pe.wait_ge(s_routeT, h + 1)
                    if e >= 6:
                        pe.wait_ge(s_hsc, dve_experts(h, e - 6))
                        pe.wait_ge(s_cbs, pool_experts(h, e - 6))
                    mm(bank(e % 6, HT), selb[:, e], routeT[:, h], start=True, stop=True).then_inc(s_cb, 1)

                for e in range(3):
                    broadcast(e)
                mm(bank(y_bank(h), HT), ebias_s[:], routeTf[:, h], start=False, stop=False)
                for e in range(EXPERTS):
                    if e + 3 < EXPERTS:
                        broadcast(e + 3)
                    if e in POOL_EXPERTS:
                        n = pool_experts(h, e)
                        pe.wait_ge(s_hsp, n)
                        src = hsp[:, n % 2]
                    else:
                        n = dve_experts(h, e)
                        pe.wait_ge(s_hsc, n)
                        src = hsc[:, n % 3]
                    for k in range(NK):
                        last = mm(bank(y_bank(h), HT), weo_s[:, e, k], src[:, k], start=False,
                                  stop=(e == EXPERTS - 1 and k == NK - 1))
                        if k == 0 and e == EXPERTS - 1:
                            pass
                    last.then_inc(s_ehid if e < EXPERTS - 1 else s_ymm, 1)


def kernel(**inputs):
    import numpy as np
    import concourse.bacc as bacc
    from concourse.bass_utils import run_bass_kernel_spmd as run

    a = {k: np.asarray(v) for k, v in inputs.items()}

    def lay(x):
        return np.ascontiguousarray(x)

    px = a["x"].reshape(IMAGES, 8, 16, 8, 16).transpose(0, 1, 3, 2, 4).reshape(HALVES, HP, K_IN, EMB)
    patches = lay(px.transpose(0, 3, 2, 1))

    def tok_w(w):
        return w.T.reshape(K_IN, EMB, EMB).transpose(1, 0, 2)

    wtok = lay(np.stack([np.stack([tok_w(a[f"L0_tok_W{n}_w"]), tok_w(a[f"L0_tok_W{n}_sw"])], 1) for n in (1, 2)], 1))
    order = np.arange(EMB).reshape(CHUNKS, DH).T.reshape(-1)
    ei1, ei2 = a["L0_tok_eps_in1"].reshape(K_IN, EMB), a["L0_tok_eps_in2"].reshape(K_IN, EMB)
    cols = lay(np.stack([
        ei1[0], ei1[1], ei2[0], ei2[1], a["L0_tok_eps_out1"], a["L0_tok_eps_out2"], a["L0_tok_W1_b"], a["L0_tok_W2_b"],
        a["L0_tok_W1_sb"], a["L0_tok_W2_sb"], a["L0_tok_W3_b"], a["L0_attn_bq"][order], a["L0_attn_bk"][order],
        a["L0_attn_bv"][order], a["L0_attn_bo"], a["L0_attn_gamma"], a["L0_attn_beta"], a["L0_ffn_ln_scale"],
        a["L0_ffn_ln_bias"], a["L0_ffn_shared_out_b"], a["cls_tok"].reshape(-1)], 1))
    eob = lay(np.concatenate([a["L0_tok_eps_out1"], a["L0_tok_eps_out2"]]))
    pos = np.arange(PATCHES, dtype=np.float32)[:, None]
    div = np.exp(np.arange(0, EMB, 2, dtype=np.float32) * np.float32(-np.log(10000.0) / EMB)).astype(np.float32)
    ang = (pos * div).astype(np.float32)
    pe = np.stack([np.sin(ang), np.cos(ang)], -1).reshape(PATCHES, EMB).astype(np.float32)
    w3pe = lay(np.concatenate([a["L0_tok_W3_w"].T, pe.T], 1))
    eye = np.eye(EMB, dtype=np.float32)
    one_nth = np.full((EMB, EMB), 1.0 / EMB, np.float32)
    stats = lay(np.stack([eye, eye - one_nth, one_nth], 1))
    wqkvo = lay(np.stack([a["L0_attn_Wq"].T[:, order], a["L0_attn_Wk"].T[:, order], a["L0_attn_Wv"].T[:, order],
                          a["L0_attn_Wo"].T[order, :]], 1))
    win = lay(np.stack([a["L0_ffn_shared_in_w"].T.reshape(EMB, 4, EMB), a["L0_ffn_expert_in_w"].T.reshape(EMB, 4, EMB)], 1))
    wso = lay(a["L0_ffn_shared_out_w"].T.reshape(NK, EMB, EMB).transpose(1, 0, 2))
    weo = lay(a["L0_ffn_expert_out_weight"].reshape(EXPERTS, EMB, NK, EMB).transpose(3, 0, 2, 1))
    gates = lay(np.concatenate([a["L0_ffn_group_gate_w"], a["L0_ffn_expert_gate_w"]], 0).T)
    tri = (np.arange(EG)[None, :] < np.arange(EG)[:, None]).astype(np.float32).reshape(-1)
    gbias = lay(np.broadcast_to(np.concatenate([a["L0_ffn_group_bias"], a["L0_ffn_expert_bias"], tri]),
                                (TOKENS, NG + EG * EG)))
    ebias = np.zeros((32, EMB), np.float32)
    ebias[24:32] = a["L0_ffn_expert_out_bias"]
    sel = np.zeros((32, EXPERTS, EMB), np.float32)
    for e in range(EXPERTS):
        sel[[e, EXPERTS + e, 2 * EXPERTS + e], e] = 1.0

    arrays = dict(cols=cols, eob=eob, patches=patches, wtok=wtok, w3pe=w3pe, stats=stats, wqkvo=wqkvo, win=win, wso=wso,
                  weo=weo, gates=gates, gbias=gbias, ebias=ebias, sel=sel)
    nc = bacc.Bacc("TRN2", target_bir_lowering=False, num_devices=1)
    args = [nc.dram_tensor(k, v.shape, F32, kind="ExternalInput").ap() for k, v in arrays.items()]
    out = nc.dram_tensor("out", (EMB, HALVES * HT), F32, kind="ExternalOutput").ap()
    vit_tower(nc, *args, out)
    r = run(nc, [arrays], core_ids=[0])
    return lay(r.results[0]["out"].T.reshape(IMAGES, TOKENS, EMB))
```

```python
from contextlib import ExitStack

import concourse.bass as bass
from concourse import mybir

EMB = 128
IMAGES = 8
PATCHES = 64
TOKENS = PATCHES + 1
PATCH_IN = 256
K_IN = PATCH_IN // EMB
HALVES = 2
HI = IMAGES // HALVES
HP = HI * PATCHES
HT = HI * TOKENS
CHUNKS = 8
DH = EMB // CHUNKS
GROUPS = 8
UG = 2
UNIT = UG * HI
UNITS = GROUPS // UG
HID = 256
NK = HID // EMB
PAIRS = 2 * NK
PAIR_ORDER = (2, 3, 0, 1)
EXPERTS = 8
EGROUPS = 2
EG = EXPERTS // EGROUPS
NG = EGROUPS + EXPERTS
BANK = 512
PART = GROUPS // 2
SCALE = float(DH) ** -0.5
EPS = 1e-5
TOPK_EPS = 1e-8
GATE_CAP = 20.0

(C_EI1, C_EI1B, C_EI2, C_EI2B, C_EO1, C_EO2, C_B1, C_B2, C_SB1, C_SB2, C_B3, C_BQ, C_BK, C_BV, C_BO, C_GAMMA,
 C_BETA, C_LNS, C_LNB, C_SOB, C_CLS) = range(21)
NCOL = 21
NEPS = 6
M_GATES, M_GBIAS = 0, NG
M_EBIAS = M_GBIAS + NG + EG * EG
M_SEL = M_EBIAS + EMB
MISC = M_SEL + EXPERTS

F32 = mybir.dt.float32
BF16 = mybir.dt.bfloat16
ALU = mybir.AluOpType
ACT = mybir.ActivationFunctionType
AX = mybir.AxisListType
ALL_UNITS = HALVES * UNITS
SIG_CAP = 2.0 ** 63
WARM = 7
WARM_REGROUP = 4
WARM_KEYS = 1
WARM_START = (1, 1, 1, 0, 2)
WARM_ROUTE = (3, 2, 2)
WARM_TAIL = 2
WARM_UNIT = 128
POOL_EXPERTS = ((2, 5), ())


def vit_tower(nc, cols, eob, patches, wtok, w3pe, stats, wqkvo, win, wso, weo, misc, out):
    with ExitStack() as ctx:
        def sb(name, shape, dt=F32):
            return ctx.enter_context(nc.sbuf_tensor(name, shape, dt))

        def sem(name):
            return ctx.enter_context(nc.semaphore(name))

        cols_s = sb("cols_s", [EMB, NCOL])
        eps_in = sb("eps_in", [EMB, NEPS + 2 * EMB])
        x_s = sb("x_s", [EMB, HALVES, K_IN, HP])
        wtok_s = sb("wtok_s", [EMB, 2, 2, K_IN, EMB])
        w3pe_s = sb("w3pe_s", [EMB, EMB + PATCHES])
        stats_s = sb("stats_s", [EMB, 3, EMB])
        ident, center, mean = stats_s[:, 0, :], stats_s[:, 1, :], stats_s[:, 2, :]
        wqkvo_s = sb("wqkvo_s", [EMB, 4, EMB])
        win_s = sb("win_s", [EMB, 2, 4, EMB])
        wso_s = sb("wso_s", [EMB, NK, EMB])
        weo_s = sb("weo_s", [EMB, EXPERTS, NK, EMB])
        misc_s = sb("misc_s", [EMB, MISC])
        gates_s = misc_s[:, M_GATES:M_GBIAS]
        gbias_s = misc_s[0:TOKENS, M_GBIAS:M_EBIAS]
        ebias_s = misc_s[0:32, M_EBIAS:M_SEL]
        sel_s = misc_s[0:32, M_SEL:MISC]
        selb = sb("selb", [32, EXPERTS, EMB], BF16)

        bias_t = sb("bias_t", [EMB, 3])
        zeros = sb("zeros", [EMB, HP])
        fabs = sb("fabs", [EMB, NEPS + 2 * EMB])
        froot = sb("froot", [EMB, NEPS + 2 * EMB])
        fsign = sb("fsign", [EMB, NEPS + 2 * EMB])
        fnoise = sb("fnoise", [EMB, NEPS + 2 * EMB])
        sig_eo = sb("sig_eo", [EMB, 2, K_IN, EMB])
        wn = sb("wn", [EMB, 2, K_IN, EMB])
        bn = sb("bn", [EMB, 2])
        gcap = sb("gcap", [EMB, HALVES, HP])
        eg = sb("eg", [EMB, HALVES, HP])
        tnum = sb("tnum", [EMB, HALVES, HP])
        tln = sb("tln", [EMB, HALVES, HP])
        trec = sb("trec", [EMB, HALVES, HP])
        gnum = sb("gnum", [EMB, HALVES, HP])
        inum = sb("inum", [EMB, HALVES, HP])
        prod = sb("prod", [EMB, HALVES, HP])
        X = sb("X", [EMB, HALVES, HI, TOKENS])
        XB = sb("XB", [EMB, HALVES, HT])
        sq = sb("sq", [EMB, 3, HALVES, HT])
        lnv = sb("lnv", [EMB, 3, HALVES, HT])
        xc = sb("xc", [EMB, 3, HALVES, HT])
        rstd = sb("rstd", [EMB, 3, HALVES, HT])
        n1 = sb("n1", [EMB, HALVES, HT])
        qkv_f = sb("qkv_f", [EMB, HALVES, HI, 3, TOKENS])
        qkv_c = sb("qkv_c", [EMB, HALVES, CHUNKS, 3, TOKENS])
        q_l = sb("q_l", [EMB, HALVES, TOKENS, CHUNKS])
        v_l = sb("v_l", [EMB, HALVES, TOKENS, CHUNKS])
        k_l = sb("k_l", [EMB, HALVES, HI, TOKENS, CHUNKS])
        v1 = sb("v1", [TOKENS, HALVES, GROUPS, HI, DH + 1])
        mx = sb("mx", [TOKENS, 2, UNIT])
        prob = sb("prob", [TOKENS, 3, UNIT, TOKENS])
        probT = sb("probT", [TOKENS, 2, UNIT, TOKENS])
        rden = sb("rden", [TOKENS, 2, UNIT])
        ctxn = sb("ctxn", [TOKENS, HALVES, GROUPS, HI, 32])
        ctx_c = sb("ctx_c", [EMB, HALVES, CHUNKS, TOKENS])
        ctx_f = sb("ctx_f", [EMB, HALVES, HI, TOKENS])
        y = sb("y", [EMB, HALVES, HT])
        z = sb("z", [EMB, HALVES, HT])
        h2 = sb("h2", [EMB, HALVES, HT])
        zf = sb("zf", [EMB, HALVES, HT])
        flat = sb("flat", [EMB, HALVES, HT])
        ea = sb("ea", [EMB, 2, HT])
        da = sb("da", [EMB, 2, HT])
        la = sb("la", [EMB, 2, HT])
        ra = sb("ra", [EMB, 2, HT])
        sa = sb("sa", [EMB, 2, HT])
        hid = sb("hid", [EMB, HALVES, PAIRS, HT])
        cb_s = sb("cb_s", [EMB, 2, HT])
        hsc = sb("hsc", [EMB, 3, NK, HT])
        hsp = sb("hsp", [EMB, 2, NK, HT])
        o_s = sb("o_s", [EMB, HALVES, HT])
        lg = sb("lg", [TOKENS, HALVES, HI, NG])
        gm = sb("gm", [TOKENS, HALVES, HI, EGROUPS])
        em = sb("em", [TOKENS, HALVES, HI, EGROUPS, EG])
        es = sb("es", [TOKENS, HALVES, HI, EG])
        emax = sb("emax", [TOKENS, HALVES, HI])
        ed = sb("ed", [TOKENS, HALVES, HI, EG])
        ee = sb("ee", [TOKENS, HALVES, HI, EG])
        esum = sb("esum", [TOKENS, HALVES, HI])
        gt = sb("gt", [TOKENS, HALVES, HI, EG * EG])
        eq = sb("eq", [TOKENS, HALVES, HI, EG * EG])
        rank = sb("rank", [TOKENS, HALVES, HI, EG])
        top = sb("top", [TOKENS, HALVES, HI, EG])
        ptop = sb("ptop", [TOKENS, HALVES, HI, EG])
        psum_top = sb("psum_top", [TOKENS, HALVES, HI])
        rtop = sb("rtop", [TOKENS, HALVES, HI])
        wtop = sb("wtop", [TOKENS, HALVES, HI, EG])
        comb = sb("comb", [TOKENS, HALVES, HI, EXPERTS])
        rest = sb("rest", [TOKENS, HALVES, HI, EXPERTS])
        route = sb("route", [TOKENS, HALVES, HI, 4, EXPERTS], BF16)
        identb = sb("identb", [EMB, EMB], BF16)
        routeT = sb("routeT", [32, HALVES, HT], BF16)
        routeTf = sb("routeTf", [32, HALVES, HT])

        PS = ctx.enter_context(nc.psum_tensor("PS", [EMB, 8, BANK], F32))
        pf = PS[:].rearrange("p b n -> p (b n)")

        def bank(b, n=BANK, rows=EMB):
            return PS[0:rows, b, 0:n]

        s_cols, s_eob, s_wtok, s_x = sem("s_cols"), sem("s_eob"), sem("s_wtok"), [sem("s_x0"), sem("s_x1")]
        s_w3pe, s_stats, s_wqkvo, s_win = sem("s_w3pe"), sem("s_stats"), sem("s_wqkvo"), sem("s_win")
        s_wso, s_weo, s_misc = sem("s_wso"), sem("s_weo"), sem("s_misc")
        s_zero, s_zk, s_ones, s_zctx, s_selb, s_identb, s_eps, s_zeros = (
            sem("s_zero"), sem("s_zk"), sem("s_ones"), sem("s_zctx"), sem("s_selb"), sem("s_identb"), sem("s_eps"), sem("s_zeros"))
        s_fabs, s_froot, s_fsign, s_fnoise = sem("s_fabs"), sem("s_froot"), sem("s_fsign"), sem("s_fnoise")
        s_sig, s_wn, s_bn = sem("s_sig"), sem("s_wn"), sem("s_bn")
        s_gate_mm, s_inner_mm, s_gcap, s_eg = sem("s_gate_mm"), sem("s_inner_mm"), sem("s_gcap"), sem("s_eg")
        s_tnum, s_tln, s_trec, s_gnum, s_inum = sem("s_tnum"), sem("s_tln"), sem("s_trec"), sem("s_gnum"), sem("s_inum")
        s_prod, s_tok_mm, s_X, s_cls, s_XB = sem("s_prod"), sem("s_tok_mm"), sem("s_X"), sem("s_cls"), sem("s_XB")
        s_cen = [sem(f"s_cen{i}") for i in range(3)]
        s_sq = [sem(f"s_sq{i}") for i in range(3)]
        s_var = [sem(f"s_var{i}") for i in range(3)]
        s_xc = [sem(f"s_xc{i}") for i in range(3)]
        s_lnv = [sem(f"s_lnv{i}") for i in range(3)]
        s_rstd = [sem(f"s_rstd{i}") for i in range(3)]
        s_n1 = sem("s_n1")
        s_qkv_mm, s_qk, s_v, s_qkvc = sem("s_qkv_mm"), sem("s_qk"), sem("s_v"), [sem("s_qkvc0"), sem("s_qkvc1")]
        s_lq, s_lk, s_lv, s_vT, s_v1 = sem("s_lq"), sem("s_lk"), sem("s_lv"), sem("s_vT"), sem("s_v1")
        s_lkd = sem("s_lkd")
        s_score, s_mx, s_sub, s_exp, s_pT, s_pTs, s_pv, s_rden, s_ctxn = (
            sem("s_score"), sem("s_mx"), sem("s_sub"), sem("s_exp"), sem("s_pT"), sem("s_pTs"), sem("s_pv"),
            sem("s_rden"), sem("s_ctxn"))
        s_ctxT, s_ctxc, s_ctxf = sem("s_ctxT"), sem("s_ctxc"), [sem("s_ctxf0"), sem("s_ctxf1")]
        s_o_mm, s_y, s_z, s_h2, s_zf, s_flat = sem("s_o_mm"), sem("s_y"), sem("s_z"), sem("s_h2"), sem("s_zf"), sem("s_flat")
        s_wtop, s_part = sem("s_wtop"), sem("s_part")
        s_lg_mm, s_route_step, s_ed, s_ee, s_route, s_routeT_mm, s_routeT, s_routeTf = (
            sem("s_lg_mm"), sem("s_route_step"), sem("s_ed"), sem("s_ee"), sem("s_route"), sem("s_routeT_mm"),
            sem("s_routeT"), sem("s_routeTf"))
        s_ab, s_ea, s_da, s_la, s_ra, s_sa, s_hid = sem("s_ab"), sem("s_ea"), sem("s_da"), sem("s_la"), sem("s_ra"), sem("s_sa"), sem("s_hid")
        s_cb, s_cbs, s_hsc, s_hsp, s_ehid, s_ymm = sem("s_cb"), sem("s_cbs"), sem("s_hsc"), sem("s_hsp"), sem("s_ehid"), sem("s_ymm")
        s_o, s_out = sem("s_o"), sem("s_out")

        def scores(n):
            b = UG * (n % 2)
            return PS[0:TOKENS, b:b + UG, 0:HT].rearrange("p g (i k) -> p g i k", k=TOKENS)

        probTs = PS[0:TOKENS, 4:4 + UG, 0:HT].rearrange("p g (i k) -> p g i k", k=TOKENS)
        pv = PS[0:TOKENS, 6, 0:UNIT * 32].rearrange("p (g d) -> p g d", d=32)
        def vT(h, part):
            return PS[0:TOKENS, (4 + part, NORM_BANK)[h]].rearrange("p (g c) -> p g c", c=EMB)

        def ctxT(h, part):
            return bank((4 + part, NORM_BANK)[1 - h], PART * TOKENS)

        NORM_BANK = 7
        ROUTE_STEPS = 12

        def gate_bank(h, net):
            return 2 * h + net

        def tok_bank(h):
            return 4 + h

        def cen_bank(h):
            return 6 + h

        def qkv_bank(h, c):
            return (2 * h, 2 * h + 1, 4 + h)[c]

        PAIR_SLOTS = (0, 1, 2, 0, 1, 0, 1, 0)

        def pair_banks(n):
            return (2 * PAIR_SLOTS[n], 2 * PAIR_SLOTS[n] + 1)

        def cb_bank(e):
            return 4 + e % 2

        def y_bank(h):
            return 6 + h

        def routeT_p(h):
            return PS[0:32, (3, NORM_BANK)[h], 0:HI * 33].bitcast(BF16).rearrange("p (i t) -> p i t", i=HI)[:, :, 0:TOKENS]

        def logits(h):
            return PS[0:TOKENS, NORM_BANK, 0:HI * 16].rearrange("p (i n) -> p i n", i=HI)[:, :, 0:NG]

        def dve_experts(h, e):
            return len([i for i in range(EXPERTS * h + e + 1) if i % EXPERTS not in POOL_EXPERTS[i // EXPERTS]])

        def pool_experts(h, e):
            return len([i for i in range(EXPERTS * h + e + 1) if i % EXPERTS in POOL_EXPERTS[i // EXPERTS]])

        def keys_of(h, images, copy, done):
            for i in images:
                rows = slice(32 * i, 32 * i + 32)
                copy(k_l[rows, h, i].rearrange("p t j -> p j t"), qkv_c[rows, h, :, 1]).then_inc(done, 1)

        def per_image(t, h):
            return t[:, h].unsqueeze(2).to_broadcast([TOKENS, HI, EG])

        def group_mask(h):
            return gm[:, h].unsqueeze(3).to_broadcast([TOKENS, HI, EGROUPS, EG])

        def both_groups(t, h):
            return t[:, h].unsqueeze(2).to_broadcast([TOKENS, HI, EGROUPS, EG])

        SQUARE = "p i (e j) -> p i e j"
        BY_GROUP = "p i (g e) -> p i g e"

        block = ctx.enter_context(nc.Block())

        @block.sync
        def _(sp):
            sp.dma_start(eps_in[:, 0:NEPS], cols[:, 0:NEPS]).then_inc(s_eob, 16)
            sp.dma_start(eps_in[:, NEPS:NEPS + 2 * EMB], eob.partition_broadcast(EMB)).then_inc(s_eob, 16)
            sp.dma_start(wtok_s[:], wtok).then_inc(s_wtok, 16)
            sp.dma_start(x_s[:, 0], patches[0]).then_inc(s_x[0], 16)
            sp.dma_start(cols_s[:], cols).then_inc(s_cols, 16)
            sp.dma_start(x_s[:, 1], patches[1]).then_inc(s_x[1], 16)
            sp.dma_start(w3pe_s[:], w3pe).then_inc(s_w3pe, 16)
            sp.dma_start(stats_s[:], stats).then_inc(s_stats, 16)
            sp.dma_start(wqkvo_s[:], wqkvo).then_inc(s_wqkvo, 16)
            sp.dma_start(misc_s[:], misc).then_inc(s_misc, 16)
            sp.dma_start(win_s[:], win).then_inc(s_win, 16)
            sp.dma_start(wso_s[:], wso).then_inc(s_wso, 16)
            sp.dma_start(weo_s[:], weo).then_inc(s_weo, 16)
            for h in range(HALVES):
                sp.wait_ge(s_qk, 2 * (h + 1))
                sp.wait_ge(s_v, h + 1)
                sp.wait_ge(s_zero, 1)
                for i in range(HI):
                    sp.dma_start(qkv_c[32 * i:32 * i + DH, h].rearrange("d j c t -> d j (c t)"),
                                 qkv_f[:, h, i].rearrange("p c t -> p (c t)")).then_inc(s_qkvc[h], 16)
            for h in range(HALVES):
                sp.wait_ge(s_ctxc, 2 * (h + 1))
                for i in range(HI):
                    sp.dma_start(ctx_f[:, h, i, :], ctx_c[32 * i:32 * i + DH, h]).then_inc(s_ctxf[h], 16)
            for h in range(HALVES):
                sp.wait_ge(s_o, h + 1)
                sp.dma_start(out[:, h * HT:(h + 1) * HT], o_s[:, h]).then_inc(s_out, 16)
            sp.wait_ge(s_out, 16 * HALVES)

        @block.gpsimd
        def _(pool):
            nc.gpsimd.memset(qkv_c[:], 0.0).then_inc(s_zero, 1)
            nc.gpsimd.memset(k_l[:, 0], 0.0).then_inc(s_zk, 1)
            nc.gpsimd.memset(v1[:], 1.0).then_inc(s_ones, 1)
            nc.gpsimd.memset(ctxn[:], 0.0).then_inc(s_zctx, 1)
            nc.gpsimd.memset(k_l[:, 1], 0.0).then_inc(s_zk, 1)
            pool.wait_ge(s_misc, 16)
            nc.gpsimd.tensor_copy(selb[:], sel_s.unsqueeze(2).to_broadcast([32, EXPERTS, EMB])).then_inc(s_selb, 1)
            pool.wait_ge(s_stats, 16)
            nc.gpsimd.tensor_copy(identb[:], ident).then_inc(s_identb, 1)
            for h in range(HALVES):
                pool.wait_ge(s_X, h + 1)
                pool.wait_ge(s_cls, 1)
                nc.gpsimd.tensor_scalar(XB[:, h], X[:, h].rearrange("p i t -> p (i t)"),
                                        cols_s[:, C_BETA:C_BETA + 1], None, ALU.add).then_inc(s_XB, 1)
            for h in range(HALVES):
                pool.wait_ge(s_qkvc[h], 16 * HI)
                nc.gpsimd.tensor_copy(v_l[:, h].rearrange("p t j -> p j t"), qkv_c[:, h, :, 2]).then_inc(s_lv, 1)

            def expert_hidden(h, e):
                n = pool_experts(h, e)
                pool.wait_ge(s_cbs, n)
                pool.wait_ge(s_hid, h * PAIRS + NK)
                if n > 2:
                    hb, eb = [(hh, i) for hh in range(HALVES) for i in POOL_EXPERTS[hh]][n - 3]
                    pool.wait_ge(s_ehid, hb * EXPERTS + eb + 1)
                nc.gpsimd.tensor_tensor(hsp[:, n % 2], hid[:, h, NK:PAIRS],
                                        cb_s[:, n % 2].unsqueeze(1).to_broadcast([EMB, NK, HT]),
                                        ALU.mult).then_inc(s_hsp, 1)

            def route_parts(h):
                pool.wait_ge(s_wtop, h + 1)
                nc.gpsimd.tensor_tensor(comb[:, h].rearrange(BY_GROUP, e=EG), both_groups(wtop, h), group_mask(h),
                                        ALU.mult).then_inc(s_part, 1)
                pool.wait_ge(s_part, 4 * h + 1)
                nc.gpsimd.tensor_copy(route[:, h, :, 0], comb[:, h]).then_inc(s_part, 1)
                pool.wait_ge(s_part, 4 * h + 2)
                nc.gpsimd.tensor_tensor(rest[:, h], comb[:, h], route[:, h, :, 0], ALU.subtract).then_inc(s_part, 1)
                pool.wait_ge(s_part, 4 * h + 3)
                nc.gpsimd.tensor_copy(route[:, h, :, 1], rest[:, h]).then_inc(s_part, 1)
                pool.wait_ge(s_part, 4 * h + 4)
                nc.gpsimd.tensor_tensor(route[:, h, :, 2], rest[:, h], route[:, h, :, 1], ALU.subtract).then_inc(s_route, 1)
                nc.gpsimd.tensor_tensor(route[:, h, :, 3].rearrange(BY_GROUP, e=EG), both_groups(top, h), group_mask(h),
                                        ALU.mult).then_inc(s_route, 1)

            route_parts(0)
            for e in POOL_EXPERTS[0]:
                expert_hidden(0, e)
            route_parts(1)
            for e in POOL_EXPERTS[1]:
                expert_hidden(1, e)

        @block.scalar
        def _(act):
            nc.scalar.preload_act_table_set("sqrt_and_others")
            act.wait_ge(s_eob, 32)
            nc.scalar.activation(fabs[:], eps_in[:], ACT.Abs).then_inc(s_fabs, 1)
            nc.scalar.activation(fsign[:], eps_in[:], ACT.Sign).then_inc(s_fsign, 1)
            act.wait_ge(s_fabs, 1)
            nc.scalar.activation(froot[:], fabs[:], ACT.Sqrt).then_inc(s_froot, 1)
            nc.scalar.preload_act_table_set("natural_log_exp_and_others")
            act.wait_ge(s_eps, 3)
            for h in range(HALVES):
                act.wait_ge(s_gcap, h + 1)
                nc.scalar.activation(eg[:, h], gcap[:, h], ACT.Exp).then_inc(s_eg, 1)
            for h in range(HALVES):
                act.wait_ge(s_tnum, h + 1)
                nc.scalar.activation(tln[:, h], tnum[:, h], ACT.Ln, bias=bias_t[:, 2:3]).then_inc(s_tln, 1)
                act.wait_ge(s_tln, h + 1)
                nc.scalar.activation(trec[:, h], tln[:, h], ACT.Exp, scale=-1.0).then_inc(s_trec, 1)

            def norm_square(use, h, b):
                act.wait_ge(s_cen[use], h + 1)
                nc.scalar.activation(sq[:, use, h], bank(b, HT), ACT.Square).then_inc(s_sq[use], 1)
                nc.scalar.copy(xc[:, use, h], bank(b, HT)).then_inc(s_xc[use], 1)

            def norm_rstd(use, h, b, scale=1.0):
                act.wait_ge(s_var[use], h + 1)
                nc.scalar.activation(lnv[:, use, h], bank(b, HT), ACT.Ln, scale=scale,
                                     bias=bias_t[:, int(use == 2):int(use == 2) + 1]).then_inc(s_lnv[use], 1)
                act.wait_ge(s_lnv[use], h + 1)
                nc.scalar.activation(rstd[:, use, h], lnv[:, use, h], ACT.Exp, scale=-0.5).then_inc(s_rstd[use], 1)

            def qk_out(h):
                for c, col in ((0, C_BQ), (1, C_BK)):
                    act.wait_ge(s_qkv_mm, 3 * h + c + 1)
                    nc.scalar.activation(qkv_f[:, h, :, c], bank(qkv_bank(h, c), HT).rearrange("p (i t) -> p i t", i=HI),
                                         ACT.Identity, bias=cols_s[:, col:col + 1]).then_inc(s_qk, 1)

            norm_square(0, 0, cen_bank(0))
            norm_rstd(0, 0, tok_bank(0))
            norm_square(0, 1, cen_bank(1))
            qk_out(0)
            norm_rstd(0, 1, tok_bank(1))
            qk_out(1)

            def values(h, part):
                act.wait_ge(s_vT, 2 * h + part + 1)
                act.wait_ge(s_ones, 1)
                nc.scalar.copy(v1[:, h, part * PART:(part + 1) * PART, :, 0:DH],
                               vT(h, part).rearrange("p g (i d) -> p g i d", d=32)[:, :, :, 0:DH]).then_inc(s_v1, 1)

            def context_out(h, part):
                act.wait_ge(s_ctxT, 2 * h + part + 1)
                src = ctxT(h, part)
                t_mid, j_mid = PART * TOKENS // CHUNKS, PART * TOKENS % CHUNKS
                if part == 0:
                    nc.scalar.copy(ctx_c[:, h, 0:j_mid, t_mid], src[:, t_mid * CHUNKS:PART * TOKENS])
                    whole, tokens = src[:, 0:t_mid * CHUNKS], slice(0, t_mid)
                else:
                    nc.scalar.copy(ctx_c[:, h, j_mid:CHUNKS, t_mid], src[:, 0:CHUNKS - j_mid])
                    whole, tokens = src[:, CHUNKS - j_mid:PART * TOKENS], slice(t_mid + 1, TOKENS)
                nc.scalar.copy(ctx_c[:, h, :, tokens].rearrange("p j t -> p t j"),
                               whole.rearrange("p (t j) -> p t j", j=CHUNKS)).then_inc(s_ctxc, 1)

            def unit_exp(n):
                act.wait_ge(s_sub, n + 1)
                nc.scalar.activation(prob[:, n % 3], prob[:, n % 3], ACT.Exp, scale=SCALE).then_inc(s_exp, 1)

            act.wait_ge(s_qkvc[0], 16 * HI)
            act.wait_ge(s_zk, 1)
            keys_of(0, (0, 1), nc.scalar.copy, s_lk)
            def tail(h, use):
                norm_square(use, h, NORM_BANK)
                norm_rstd(use, h, NORM_BANK, 1.0 if use == 1 else 1.0 + EPS)

            unit_exp(0)
            values(0, 0)
            values(0, 1)
            unit_exp(1)
            for n in range(ALL_UNITS):
                act.wait_ge(s_pT, n + 1)
                if n >= 2:
                    act.wait_ge(s_pv, n - 1)
                nc.scalar.copy(probT[:, n % 2].rearrange("p (g i) k -> p g i k", g=UG), probTs).then_inc(s_pTs, 1)
                if n == 0:
                    act.wait_ge(s_qkvc[1], 16 * HI)
                    act.wait_ge(s_zk, 2)
                    keys_of(1, (0,), nc.scalar.copy, s_lk)
                if n == 1:
                    keys_of(1, (1,), nc.scalar.copy, s_lk)
                if n == 2:
                    values(1, 1)
                if n == 4:
                    context_out(0, 1)
                if n + 2 < ALL_UNITS:
                    unit_exp(n + 2)
                if n == 1:
                    values(1, 0)
                if n == 3:
                    context_out(0, 0)
            norm_square(1, 0, NORM_BANK)
            norm_rstd(1, 0, NORM_BANK)
            context_out(1, 0)
            context_out(1, 1)

            def pair_sigmoid(h, q):
                n = h * PAIRS + q
                act.wait_ge(s_da, n + 1)
                nc.scalar.activation(la[:, n % 2], da[:, n % 2], ACT.Ln).then_inc(s_la, 1)
                act.wait_ge(s_la, n + 1)
                if n >= 2:
                    act.wait_ge(s_sa, n - 1)
                nc.scalar.activation(ra[:, n % 2], la[:, n % 2], ACT.Exp, scale=-1.0).then_inc(s_ra, 1)

            def pair_exp(h, q):
                n = h * PAIRS + q
                act.wait_ge(s_ab, n + 1)
                if n >= 2:
                    act.wait_ge(s_da, n - 1)
                nc.scalar.activation(ea[:, n % 2], bank(pair_banks(n)[0], HT), ACT.Exp, scale=-1.0).then_inc(s_ea, 1)

            def router_exp(h):
                act.wait_ge(s_ed, h + 1)
                nc.scalar.activation(ee[:, h], ed[:, h], ACT.Exp).then_inc(s_ee, 1)

            def route_out(h):
                act.wait_ge(s_routeT_mm, h + 1)
                for t, done in ((routeT, s_routeT), (routeTf, s_routeTf)):
                    nc.scalar.copy(t[:, h].rearrange("p (i t) -> p i t", i=HI), routeT_p(h)).then_inc(done, 1)

            def broadcast_out(h, e):
                n = pool_experts(h, e)
                act.wait_ge(s_cb, h * EXPERTS + e + 1)
                if n > 2:
                    act.wait_ge(s_hsp, n - 2)
                nc.scalar.copy(cb_s[:, n % 2], bank(cb_bank(e), HT)).then_inc(s_cbs, 1)

            tail(0, 2)
            pair_exp(0, 0)
            pair_exp(0, 1)
            router_exp(0)
            pair_sigmoid(0, 0)
            pair_sigmoid(0, 1)
            pair_exp(0, 2)
            pair_sigmoid(0, 2)
            norm_square(1, 1, NORM_BANK)
            pair_exp(0, 3)
            norm_rstd(1, 1, NORM_BANK)
            route_out(0)
            pair_sigmoid(0, 3)
            broadcast_out(0, POOL_EXPERTS[0][0])
            norm_square(2, 1, NORM_BANK)
            norm_rstd(2, 1, NORM_BANK, 1.0 + EPS)
            broadcast_out(0, POOL_EXPERTS[0][1])
            pair_exp(1, 0)
            router_exp(1)
            pair_exp(1, 1)
            pair_sigmoid(1, 0)
            pair_sigmoid(1, 1)
            pair_exp(1, 2)
            route_out(1)
            pair_sigmoid(1, 2)
            pair_exp(1, 3)
            pair_sigmoid(1, 3)
            for e in POOL_EXPERTS[1]:
                broadcast_out(1, e)

        @block.vector
        def _(dve):
            step = [0]

            def routed(ins):
                step[0] += 1
                ins.then_inc(s_route_step, 1)

            def last_step():
                dve.wait_ge(s_route_step, step[0])

            nc.vector.memset(zeros[:], 0.0).then_inc(s_zeros, 1)
            nc.vector.memset(bias_t[:, 0:1], EPS).then_inc(s_eps, 1)
            nc.vector.memset(bias_t[:, 1:2], EPS * EPS).then_inc(s_eps, 1)
            nc.vector.memset(bias_t[:, 2:3], 2.0).then_inc(s_eps, 1)
            dve.wait_ge(s_froot, 1)
            dve.wait_ge(s_fsign, 1)
            nc.vector.tensor_tensor(fnoise[:], froot[:], fsign[:], ALU.mult).then_inc(s_fnoise, 1)
            dve.wait_ge(s_fnoise, 1)
            dve.wait_ge(s_wtok, 16)
            for net in range(2):
                nc.vector.tensor_tensor(sig_eo[:, net], wtok_s[:, net, 1],
                                        fnoise[:, NEPS + net * EMB:NEPS + (net + 1) * EMB].unsqueeze(1)
                                        .to_broadcast([EMB, K_IN, EMB]), ALU.mult).then_inc(s_sig, 1)
                dve.wait_ge(s_sig, net + 1)
                for k in range(K_IN):
                    c = 2 * net + k
                    nc.vector.scalar_tensor_tensor(out=wn[:, net, k], in0=sig_eo[:, net, k],
                                                   scalar=fnoise[:, c:c + 1], in1=wtok_s[:, net, 0, k],
                                                   op0=ALU.mult, op1=ALU.add).then_inc(s_wn, 1)
            dve.wait_ge(s_cols, 16)
            for net in range(2):
                nc.vector.scalar_tensor_tensor(out=bn[:, net:net + 1], in0=cols_s[:, C_SB1 + net:C_SB1 + net + 1],
                                               scalar=fnoise[:, C_EO1 + net:C_EO1 + net + 1],
                                               in1=cols_s[:, C_B1 + net:C_B1 + net + 1],
                                               op0=ALU.mult, op1=ALU.add).then_inc(s_bn, 1)
            nc.vector.tensor_copy(X[:, :, :, 0:1], cols_s[:, C_CLS:C_CLS + 1].unsqueeze(1).unsqueeze(1)
                                  .to_broadcast([EMB, HALVES, HI, 1])).then_inc(s_cls, 1)
            dve.wait_ge(s_bn, 2)
            for h in range(HALVES):
                dve.wait_ge(s_gate_mm, h + 1)
                nc.vector.tensor_scalar(gcap[:, h], bank(gate_bank(h, 0), HP), bn[:, 0:1], GATE_CAP, ALU.add,
                                        ALU.min).then_inc(s_gcap, 1)

            def gate_start(h):
                dve.wait_ge(s_eg, h + 1)
                nc.vector.scalar_tensor_tensor(out=tnum[:, h], in0=eg[:, h], scalar=2.0, in1=eg[:, h],
                                               op0=ALU.add, op1=ALU.mult).then_inc(s_tnum, 1)

            def gate_product(h):
                dve.wait_ge(s_tnum, h + 1)
                nc.vector.scalar_tensor_tensor(out=gnum[:, h], in0=bank(gate_bank(h, 0), HP), scalar=bn[:, 0:1],
                                               in1=tnum[:, h], op0=ALU.add, op1=ALU.mult).then_inc(s_gnum, 1)
                dve.wait_ge(s_inner_mm, h + 1)
                dve.wait_ge(s_gnum, h + 1)
                nc.vector.scalar_tensor_tensor(out=inum[:, h], in0=bank(gate_bank(h, 1), HP), scalar=bn[:, 1:2],
                                               in1=gnum[:, h], op0=ALU.add, op1=ALU.mult).then_inc(s_inum, 1)
                dve.wait_ge(s_trec, h + 1)
                dve.wait_ge(s_inum, h + 1)
                nc.vector.tensor_tensor(prod[:, h], inum[:, h], trec[:, h], ALU.mult).then_inc(s_prod, 1)

            def tokens(h):
                dve.wait_ge(s_tok_mm, h + 1)
                nc.vector.scalar_tensor_tensor(
                    out=X[:, h, :, 1:TOKENS], in0=bank(tok_bank(h), HP).rearrange("p (i t) -> p i t", i=HI),
                    scalar=cols_s[:, C_B3:C_B3 + 1],
                    in1=w3pe_s[:, EMB:EMB + PATCHES].unsqueeze(1).to_broadcast([EMB, HI, PATCHES]),
                    op0=ALU.add, op1=ALU.add).then_inc(s_X, 1)

            def norm_rows(h):
                dve.wait_ge(s_rstd[0], h + 1)
                dve.wait_ge(s_xc[0], h + 1)
                nc.vector.tensor_tensor(n1[:, h], xc[:, 0, h], rstd[:, 0, h], ALU.mult).then_inc(s_n1, 1)

            def value_out(h):
                dve.wait_ge(s_qkv_mm, 3 * h + 3)
                nc.vector.tensor_scalar(qkv_f[:, h, :, 2], bank(qkv_bank(h, 2), HT).rearrange("p (i t) -> p i t", i=HI),
                                        cols_s[:, C_BV:C_BV + 1], None, ALU.add).then_inc(s_v, 1)

            gate_start(0)
            gate_product(0)
            gate_start(1)
            dve.wait_ge(s_w3pe, 16)
            tokens(0)
            gate_product(1)
            tokens(1)
            norm_rows(0)
            value_out(0)
            norm_rows(1)
            value_out(1)

            def queries(h):
                dve.wait_ge(s_qkvc[h], 16 * HI)
                nc.vector.tensor_copy(q_l[:, h].rearrange("p t j -> p j t"), qkv_c[:, h, :, 0]).then_inc(s_lq, 1)

            queries(0)
            dve.wait_ge(s_zk, 1)
            keys_of(0, (2, 3), nc.vector.tensor_copy, s_lkd)

            def softmax_shift(n):
                dve.wait_ge(s_score, n + 1)
                nc.vector.tensor_reduce(mx[:, n % 2].rearrange("p (g i) -> p g i", g=UG), scores(n), AX.X,
                                        ALU.max).then_inc(s_mx, 1)
                dve.wait_ge(s_mx, n + 1)
                if n >= 3:
                    dve.wait_ge(s_pT, n - 2)
                nc.vector.tensor_tensor(prob[:, n % 3].rearrange("p (g i) k -> p g i k", g=UG), scores(n),
                                        mx[:, n % 2].rearrange("p (g i) -> p g i", g=UG).unsqueeze(3)
                                        .to_broadcast([TOKENS, UG, HI, TOKENS]), ALU.subtract).then_inc(s_sub, 1)

            def context_norm(n):
                h, u = n // UNITS, n % UNITS
                dve.wait_ge(s_pv, n + 1)
                nc.vector.reciprocal(rden[:, n % 2], pv[:, :, DH]).then_inc(s_rden, 1)
                dve.wait_ge(s_rden, n + 1)
                nc.vector.tensor_tensor(
                    ctxn[:, h, UG * u:UG * u + UG, :, 0:DH],
                    pv[:, :, 0:DH].rearrange("p (g i) d -> p g i d", g=UG),
                    rden[:, n % 2].rearrange("p (g i) -> p g i", g=UG).unsqueeze(3)
                    .to_broadcast([TOKENS, UG, HI, DH]), ALU.mult).then_inc(s_ctxn, 1)

            def residual(h):
                dve.wait_ge(s_o_mm, h + 1)
                nc.vector.scalar_tensor_tensor(out=y[:, h], in0=bank(NORM_BANK, HT), scalar=cols_s[:, C_BO:C_BO + 1],
                                               in1=n1[:, h], op0=ALU.add, op1=ALU.add).then_inc(s_y, 1)

            def hidden_rows(h):
                dve.wait_ge(s_rstd[1], h + 1)
                dve.wait_ge(s_xc[1], h + 1)
                nc.vector.tensor_tensor(z[:, h], xc[:, 1, h], rstd[:, 1, h], ALU.mult).then_inc(s_z, 1)
                dve.wait_ge(s_z, h + 1)
                dve.wait_ge(s_XB, h + 1)
                nc.vector.scalar_tensor_tensor(out=h2[:, h], in0=z[:, h], scalar=cols_s[:, C_GAMMA:C_GAMMA + 1],
                                               in1=XB[:, h], op0=ALU.mult, op1=ALU.add).then_inc(s_h2, 1)

            def flat_rows(h):
                dve.wait_ge(s_rstd[2], h + 1)
                dve.wait_ge(s_xc[2], h + 1)
                nc.vector.tensor_tensor(zf[:, h], xc[:, 2, h], rstd[:, 2, h], ALU.mult).then_inc(s_zf, 1)
                dve.wait_ge(s_zf, h + 1)
                nc.vector.tensor_scalar(flat[:, h], zf[:, h], cols_s[:, C_LNS:C_LNS + 1],
                                        cols_s[:, C_LNB:C_LNB + 1], ALU.mult, ALU.add).then_inc(s_flat, 1)

            def router_logits(h):
                dve.wait_ge(s_lg_mm, h + 1)
                routed(nc.vector.tensor_tensor(
                    lg[:, h], logits(h),
                    gbias_s[:, 0:NG].unsqueeze(1).to_broadcast([TOKENS, HI, NG]), ALU.add))
                last_step()
                nc.vector.tensor_tensor(gm[:, h, :, 0:1], lg[:, h, :, 0:1], lg[:, h, :, 1:2], ALU.is_ge)
                routed(nc.vector.tensor_tensor(gm[:, h, :, 1:2], lg[:, h, :, 0:1], lg[:, h, :, 1:2], ALU.is_lt))

            def router_group(h):
                last_step()
                routed(nc.vector.tensor_tensor(em[:, h], lg[:, h, :, EGROUPS:NG].rearrange("p i (g e) -> p i g e", e=EG),
                                               group_mask(h), ALU.mult))
                last_step()
                routed(nc.vector.tensor_tensor(es[:, h], em[:, h, :, 0], em[:, h, :, 1], ALU.add))

            def router_shift(h):
                last_step()
                routed(nc.vector.tensor_reduce(emax[:, h], es[:, h], AX.X, ALU.max))
                last_step()
                nc.vector.tensor_tensor(ed[:, h], es[:, h], per_image(emax, h), ALU.subtract).then_inc(s_ed, 1)

            def router_compare(h):
                l_j = es[:, h].unsqueeze(2).to_broadcast([TOKENS, HI, EG, EG])
                l_e = es[:, h].unsqueeze(3).to_broadcast([TOKENS, HI, EG, EG])
                nc.vector.tensor_tensor(gt[:, h].rearrange(SQUARE, e=EG), l_j, l_e, ALU.is_gt)
                routed(nc.vector.tensor_tensor(eq[:, h].rearrange(SQUARE, e=EG), l_j, l_e, ALU.is_equal))

            def router_ties(h):
                last_step()
                routed(nc.vector.tensor_tensor(eq[:, h], eq[:, h],
                                               gbias_s[:, NG:NG + EG * EG].unsqueeze(1)
                                               .to_broadcast([TOKENS, HI, EG * EG]), ALU.mult))
                last_step()
                routed(nc.vector.tensor_tensor(gt[:, h], gt[:, h], eq[:, h], ALU.add))

            def router_rank(h):
                last_step()
                routed(nc.vector.tensor_reduce(rank[:, h], gt[:, h].rearrange(SQUARE, e=EG), AX.X, ALU.add))

            def router_top(h):
                last_step()
                dve.wait_ge(s_ee, h + 1)
                nc.vector.tensor_reduce(esum[:, h], ee[:, h], AX.X, ALU.add)
                nc.vector.tensor_single_scalar(top[:, h], rank[:, h], 1.5, ALU.is_lt)
                routed(nc.vector.scalar_tensor_tensor(out=ptop[:, h], in0=rank[:, h], scalar=1.5, in1=ee[:, h],
                                                      op0=ALU.is_lt, op1=ALU.mult))

            def router_norm(h):
                last_step()
                routed(nc.vector.tensor_reduce(psum_top[:, h], ptop[:, h], AX.X, ALU.add))
                last_step()
                routed(nc.vector.scalar_tensor_tensor(out=psum_top[:, h], in0=esum[:, h], scalar=TOPK_EPS,
                                                      in1=psum_top[:, h], op0=ALU.mult, op1=ALU.add))

            def router_weights(h):
                last_step()
                routed(nc.vector.reciprocal(rtop[:, h], psum_top[:, h]))
                last_step()
                nc.vector.tensor_tensor(wtop[:, h], ptop[:, h], per_image(rtop, h), ALU.mult).then_inc(s_wtop, 1)

            def sigmoid_sum(n):
                dve.wait_ge(s_ea, n + 1)
                if n >= 2:
                    dve.wait_ge(s_la, n - 1)
                nc.vector.tensor_scalar(da[:, n % 2], ea[:, n % 2], SIG_CAP, 1.0, ALU.min,
                                        ALU.add).then_inc(s_da, 1)

            def swiglu(n):
                h, q = n // PAIRS, PAIR_ORDER[n % PAIRS]
                a, b = (bank(x, HT) for x in pair_banks(n))
                dve.wait_ge(s_ra, n + 1)
                nc.vector.tensor_tensor(sa[:, n % 2], a, ra[:, n % 2], ALU.mult).then_inc(s_sa, 1)
                dve.wait_ge(s_sa, n + 1)
                nc.vector.tensor_tensor(hid[:, h, q], b, sa[:, n % 2], ALU.mult).then_inc(s_hid, 1)

            def expert_hidden(h, e):
                if e in POOL_EXPERTS[h]:
                    return
                n = dve_experts(h, e)
                dve.wait_ge(s_hid, h * PAIRS + NK)
                dve.wait_ge(s_cb, h * EXPERTS + e + 1)
                if n > 3:
                    hb, eb = [(hh, i) for hh in range(HALVES) for i in range(EXPERTS) if i not in POOL_EXPERTS[hh]][n - 4]
                    dve.wait_ge(s_ehid, hb * EXPERTS + eb + 1)
                nc.vector.tensor_tensor(hsc[:, n % 3], hid[:, h, NK:PAIRS],
                                        bank(cb_bank(e), HT).unsqueeze(1).to_broadcast([EMB, NK, HT]),
                                        ALU.mult).then_inc(s_hsc, 1)

            def result(h):
                dve.wait_ge(s_ehid, (h + 1) * EXPERTS)
                nc.vector.scalar_tensor_tensor(out=o_s[:, h], in0=bank(y_bank(h), HT), scalar=cols_s[:, C_SOB:C_SOB + 1],
                                               in1=h2[:, h], op0=ALU.add, op1=ALU.add).then_inc(s_o, 1)

            dve.wait_ge(s_zctx, 1)
            softmax_shift(0)
            softmax_shift(1)
            for n in range(ALL_UNITS):
                if n + 2 < ALL_UNITS:
                    softmax_shift(n + 2)
                if n == 6:
                    residual(0)
                context_norm(n)
                if n == 0:
                    queries(1)
                    dve.wait_ge(s_zk, 2)
                    keys_of(1, (2,), nc.vector.tensor_copy, s_lkd)
                if n == 1:
                    keys_of(1, (3,), nc.vector.tensor_copy, s_lkd)
            hidden_rows(0)
            flat_rows(0)
            router_logits(0)
            router_group(0)
            router_shift(0)
            sigmoid_sum(0)
            router_compare(0)
            sigmoid_sum(1)
            router_ties(0)
            router_rank(0)
            swiglu(0)
            router_top(0)
            residual(1)
            router_norm(0)
            sigmoid_sum(2)
            router_weights(0)
            swiglu(1)
            sigmoid_sum(3)
            swiglu(2)
            hidden_rows(1)
            expert_hidden(0, 0)
            expert_hidden(0, 1)
            swiglu(3)
            flat_rows(1)
            expert_hidden(0, 3)
            router_logits(1)
            router_group(1)
            router_shift(1)
            router_compare(1)
            sigmoid_sum(4)
            router_ties(1)
            router_rank(1)
            expert_hidden(0, 4)
            router_top(1)
            sigmoid_sum(5)
            router_norm(1)
            router_weights(1)
            swiglu(4)
            expert_hidden(0, 6)
            swiglu(5)
            expert_hidden(0, 7)
            sigmoid_sum(6)
            expert_hidden(1, 0)
            expert_hidden(1, 1)
            swiglu(6)
            result(0)
            sigmoid_sum(7)
            expert_hidden(1, 2)
            expert_hidden(1, 3)
            swiglu(7)
            for e in range(4, EXPERTS):
                expert_hidden(1, e)
            result(1)

        @block.tensor
        def _(pe):
            mm = nc.tensor.matmul
            pe.wait_ge(s_zeros, 1)

            def keep_warm(count, b=NORM_BANK, n=HP):
                for _w in range(count):
                    mm(bank(b, n), zeros[:, 0:EMB], zeros[:, 0:n], start=True, stop=True)

            keep_warm(WARM)
            pe.wait_ge(s_wn, 4)
            for h in range(HALVES):
                pe.wait_ge(s_x[h], 16)
                for net, done in ((0, s_gate_mm), (1, s_inner_mm)):
                    for k in range(K_IN):
                        last = mm(bank(gate_bank(h, net), HP), wn[:, net, k], x_s[:, h, k], start=(k == 0),
                                  stop=(k == K_IN - 1))
                    last.then_inc(done, 1)
            pe.wait_ge(s_w3pe, 16)
            pe.wait_ge(s_stats, 16)
            pe.wait_ge(s_wqkvo, 16)

            def embed(h):
                pe.wait_ge(s_prod, h + 1)
                mm(bank(tok_bank(h), HP), w3pe_s[:, 0:EMB], prod[:, h], start=True, stop=True).then_inc(s_tok_mm, 1)

            def norm_center(use, h, b, rows):
                mm(bank(b, HT), center, rows, start=True, stop=True).then_inc(s_cen[use], 1)

            def norm_var(use, h, b):
                pe.wait_ge(s_sq[use], h + 1)
                pe.wait_ge(s_xc[use], h + 1)
                mm(bank(b, HT), mean, sq[:, use, h], start=True, stop=True).then_inc(s_var[use], 1)

            def center_tokens(h):
                pe.wait_ge(s_cls, 1)
                pe.wait_ge(s_X, h + 1)
                norm_center(0, h, cen_bank(h), X[:, h].rearrange("p i t -> p (i t)"))

            def project(h):
                pe.wait_ge(s_n1, h + 1)
                for c in range(3):
                    mm(bank(qkv_bank(h, c), HT), wqkvo_s[:, c], n1[:, h], start=True, stop=True).then_inc(s_qkv_mm, 1)

            keep_warm(WARM_START[0], cen_bank(1))
            embed(0)
            keep_warm(WARM_START[1], cen_bank(1))
            center_tokens(0)
            keep_warm(WARM_START[2], cen_bank(1))
            norm_var(0, 0, tok_bank(0))
            embed(1)
            center_tokens(1)
            keep_warm(WARM_START[3], cen_bank(0))
            project(0)
            norm_var(0, 1, tok_bank(1))
            keep_warm(WARM_START[4], cen_bank(0))
            project(1)

            def unit_place(n):
                return n // UNITS, UG * (n % UNITS)

            def unit_scores(n):
                h, g0 = unit_place(n)
                if n >= 2:
                    pe.wait_ge(s_sub, n - 1)
                if n % UNITS == 0:
                    pe.wait_ge(s_lq, h + 1)
                    pe.wait_ge(s_lk, 2 * (h + 1))
                    pe.wait_ge(s_lkd, 2 * (h + 1))
                q_h = q_l[:, h].rearrange("p t j -> p (t j)")
                k_h = k_l[:, h].rearrange("p i t j -> p i (t j)")
                for g in range(UG):
                    chunk = slice((g0 + g) * TOKENS, (g0 + g + 1) * TOKENS)
                    last = mm(scores(n)[:, g], q_h[:, chunk], k_h[:, :, chunk], start=True, stop=True)
                last.then_inc(s_score, 1)

            def unit_transposes(n):
                pe.wait_ge(s_exp, n + 1)
                if n >= 1:
                    pe.wait_ge(s_pTs, n)
                if n == 0:
                    pe.wait_ge(s_v1, 2)
                for g in range(UNIT):
                    last = nc.tensor.transpose(probTs[:, g // HI, g % HI], prob[:, n % 3, g], ident[0:TOKENS, 0:TOKENS])
                last.then_inc(s_pT, 1)

            def unit_context(n):
                h, g0 = unit_place(n)
                pe.wait_ge(s_pTs, n + 1)
                if n == UNITS:
                    pe.wait_ge(s_v1, 4)
                if n >= 1:
                    pe.wait_ge(s_ctxn, n)
                for g in range(UNIT):
                    last = mm(pv[:, g, 0:DH + 1], probT[:, n % 2, g], v1[:, h, g0 + g // HI, g % HI],
                              start=True, stop=True)
                last.then_inc(s_pv, 1)

            def values(h, part):
                if part == 0:
                    pe.wait_ge(s_lv, h + 1)
                if h == 1:
                    if part == 1:
                        pe.wait_ge(s_v1, 3)
                v_h = v_l[:, h].rearrange("p t j -> p (t j)")
                for g in range(PART):
                    chunk = (part * PART + g) * TOKENS
                    last = nc.tensor.transpose(vT(h, part)[:, g], v_h[:, chunk:chunk + TOKENS], ident)
                last.then_inc(s_vT, 1)

            def context_images(h, part):
                pe.wait_ge(s_ctxn, h * UNITS + (part + 1) * UNITS // 2)
                if h == 0:
                    if part == 0:
                        pe.wait_ge(s_v1, 4)
                    else:
                        pe.wait_ge(s_ctxc, 1)
                if h == 1:
                    pe.wait_ge(s_pTs, ALL_UNITS)
                for g in range(PART):
                    last = nc.tensor.transpose(ctxT(h, part)[:, g * TOKENS:(g + 1) * TOKENS],
                                               ctxn[:, h, part * PART + g].rearrange("p i d -> p (i d)"),
                                               ident[0:TOKENS, 0:TOKENS])
                last.then_inc(s_ctxT, 1)

            keep_warm(WARM_REGROUP)
            pe.wait_ge(s_qk, 4)
            pe.wait_ge(s_v, 2)
            unit_scores(0)
            unit_scores(1)
            keep_warm(WARM_KEYS)
            values(0, 0)
            values(0, 1)

            def attend_out(h):
                pe.wait_ge(s_ctxf[h], 16 * HI)
                if h == 0:
                    pe.wait_ge(s_ctxc, 2)
                else:
                    pe.wait_ge(s_route_step, 1)
                mm(bank(NORM_BANK, HT), wqkvo_s[:, 3], ctx_f[:, h].rearrange("p i t -> p (i t)"), start=True,
                   stop=True).then_inc(s_o_mm, 1)

            def center_attended(h):
                pe.wait_ge(s_y, h + 1)
                norm_center(1, h, NORM_BANK, y[:, h])

            def center_hidden(h):
                pe.wait_ge(s_h2, h + 1)
                norm_center(2, h, NORM_BANK, h2[:, h])

            def gate_logits(h):
                pe.wait_ge(s_flat, h + 1)
                for i in range(HI):
                    last = mm(logits(h)[:, i], flat[:, h, i * TOKENS:(i + 1) * TOKENS], gates_s, start=True, stop=True)
                last.then_inc(s_lg_mm, 1)

            def pair(h, m):
                n = h * PAIRS + m
                before = [k for k in range(n) if PAIR_SLOTS[k] == PAIR_SLOTS[n]]
                if before:
                    pe.wait_ge(s_hid, before[-1] + 1)
                q = PAIR_ORDER[m]
                for ab, b in zip(range(2), pair_banks(n)):
                    last = mm(bank(b, HT), win_s[:, q // NK, NK * ab + q % NK], flat[:, h], start=True, stop=True)
                last.then_inc(s_ab, 1)

            def bias_out(h):
                pe.wait_ge(s_routeTf, h + 1)
                mm(bank(y_bank(h), HT), ebias_s, routeTf[:, h], start=True, stop=False)

            def shared_out(h):
                pe.wait_ge(s_hid, (h + 1) * PAIRS)
                for k in range(NK):
                    mm(bank(y_bank(h), HT), wso_s[:, k], hid[:, h, k], start=False, stop=False)

            def route_transposes(h):
                pe.wait_ge(s_route, 2 * (h + 1))
                if h == 0:
                    pe.wait_ge(s_hid, 2)
                else:
                    pe.wait_ge(s_route_step, ROUTE_STEPS + 1)
                for i in range(HI):
                    last = nc.tensor.transpose(routeT_p(h)[:, i], route[:, h, i].rearrange("p a e -> p (a e)"),
                                               identb[0:TOKENS, 0:TOKENS])
                last.then_inc(s_routeT_mm, 1)

            def broadcast(h, e):
                if e == 0:
                    pe.wait_ge(s_routeT, h + 1)
                    pe.wait_ge(s_hid, 3)
                behind = [m for m in range(h * EXPERTS + e) if cb_bank(m % EXPERTS) == cb_bank(e)]
                if behind:
                    hb, eb = behind[-1] // EXPERTS, behind[-1] % EXPERTS
                    if eb in POOL_EXPERTS[hb]:
                        pe.wait_ge(s_cbs, pool_experts(hb, eb))
                    else:
                        pe.wait_ge(s_hsc, dve_experts(hb, eb))
                mm(bank(cb_bank(e), HT), selb[:, e], routeT[:, h], start=True, stop=True).then_inc(s_cb, 1)

            def expert_out(h, e):
                if e in POOL_EXPERTS[h]:
                    n = pool_experts(h, e)
                    pe.wait_ge(s_hsp, n)
                    src = hsp[:, n % 2]
                else:
                    n = dve_experts(h, e)
                    pe.wait_ge(s_hsc, n)
                    src = hsc[:, n % 3]
                for k in range(NK):
                    last = mm(bank(y_bank(h), HT), weo_s[:, e, k], src[:, k], start=False,
                              stop=(e == EXPERTS - 1 and k == NK - 1))
                last.then_inc(s_ehid, 1)

            for n in range(ALL_UNITS):
                if n >= 1:
                    keep_warm(1, 4, WARM_UNIT)
                unit_transposes(n)
                if n + 2 < ALL_UNITS:
                    unit_scores(n + 2)
                if n == 1:
                    values(1, 0)
                if n == 2:
                    values(1, 1)
                if n == 3:
                    context_images(0, 0)
                if n == 4:
                    context_images(0, 1)
                if n == 6:
                    keep_warm(1, 0)
                    attend_out(0)
                if n == 7:
                    keep_warm(1, 0)
                    center_attended(0)
                unit_context(n)
            keep_warm(1, 0)
            norm_var(1, 0, NORM_BANK)
            context_images(1, 0)
            context_images(1, 1)
            keep_warm(2 * WARM_TAIL, 0)
            center_hidden(0)
            keep_warm(WARM_TAIL, 0)
            norm_var(2, 0, NORM_BANK)
            keep_warm(2 * WARM_TAIL, 0)
            pe.wait_ge(s_misc, 16)
            gate_logits(0)
            pe.wait_ge(s_win, 16)
            pe.wait_ge(s_wso, 16)
            pe.wait_ge(s_weo, 16)
            pe.wait_ge(s_selb, 1)
            pe.wait_ge(s_identb, 1)
            pe.wait_ge(s_ctxn, ALL_UNITS)
            pe.wait_ge(s_ctxc, 4)
            pair(0, 0)
            pair(0, 1)
            pair(0, 2)
            attend_out(1)
            keep_warm(WARM_ROUTE[0], y_bank(0))
            pair(0, 3)
            center_attended(1)
            keep_warm(WARM_ROUTE[1], y_bank(0))
            norm_var(1, 1, NORM_BANK)
            route_transposes(0)
            keep_warm(WARM_ROUTE[2], y_bank(0))
            broadcast(0, 0)
            broadcast(0, 1)
            bias_out(0)
            center_hidden(1)
            for e in range(EXPERTS):
                if e + 2 < EXPERTS:
                    broadcast(0, e + 2)
                if e == 6:
                    pair(1, 2)
                expert_out(0, e)
                if e == 0:
                    norm_var(2, 1, NORM_BANK)
                if e == 1:
                    shared_out(0)
                if e == 2:
                    gate_logits(1)
                    pair(1, 0)
                if e == 3:
                    pair(1, 1)
                if e == 6:
                    route_transposes(1)
            broadcast(1, 0)
            broadcast(1, 1)
            bias_out(1)
            for e in range(EXPERTS):
                if e + 2 < EXPERTS:
                    broadcast(1, e + 2)
                expert_out(1, e)
                if e == 0:
                    pair(1, 3)
                if e == 4:
                    shared_out(1)


def kernel(**inputs):
    import numpy as np
    import concourse.bacc as bacc
    from concourse.bass_utils import run_bass_kernel_spmd as run

    a = {k: np.asarray(v) for k, v in inputs.items()}

    def lay(x):
        return np.ascontiguousarray(x)

    px = a["x"].reshape(IMAGES, 8, 16, 8, 16).transpose(0, 1, 3, 2, 4).reshape(HALVES, HP, K_IN, EMB)
    patches = lay(px.transpose(0, 3, 2, 1))

    def tok_w(w):
        return w.T.reshape(K_IN, EMB, EMB).transpose(1, 0, 2)

    wtok = lay(np.stack([np.stack([tok_w(a[f"L0_tok_W{n}_w"]), tok_w(a[f"L0_tok_W{n}_sw"])], 1) for n in (1, 2)], 1))
    order = np.arange(EMB).reshape(CHUNKS, DH).T.reshape(-1)
    ei1, ei2 = a["L0_tok_eps_in1"].reshape(K_IN, EMB), a["L0_tok_eps_in2"].reshape(K_IN, EMB)
    cols = lay(np.stack([
        ei1[0], ei1[1], ei2[0], ei2[1], a["L0_tok_eps_out1"], a["L0_tok_eps_out2"], a["L0_tok_W1_b"], a["L0_tok_W2_b"],
        a["L0_tok_W1_sb"], a["L0_tok_W2_sb"], a["L0_tok_W3_b"], a["L0_attn_bq"][order], a["L0_attn_bk"][order],
        a["L0_attn_bv"][order], a["L0_attn_bo"], a["L0_attn_gamma"], a["L0_attn_beta"], a["L0_ffn_ln_scale"],
        a["L0_ffn_ln_bias"], a["L0_ffn_shared_out_b"], a["cls_tok"].reshape(-1)], 1))
    eob = lay(np.concatenate([a["L0_tok_eps_out1"], a["L0_tok_eps_out2"]]))
    pos = np.arange(PATCHES, dtype=np.float32)[:, None]
    div = np.exp(np.arange(0, EMB, 2, dtype=np.float32) * np.float32(-np.log(10000.0) / EMB)).astype(np.float32)
    ang = (pos * div).astype(np.float32)
    pe = np.stack([np.sin(ang), np.cos(ang)], -1).reshape(PATCHES, EMB).astype(np.float32)
    w3pe = lay(np.concatenate([a["L0_tok_W3_w"].T, pe.T], 1))
    eye = np.eye(EMB, dtype=np.float32)
    one_nth = np.full((EMB, EMB), 1.0 / EMB, np.float32)
    stats = lay(np.stack([eye, eye - one_nth, one_nth], 1))
    wqkvo = lay(np.stack([a["L0_attn_Wq"].T[:, order], a["L0_attn_Wk"].T[:, order], a["L0_attn_Wv"].T[:, order],
                          a["L0_attn_Wo"].T[order, :]], 1))
    win = lay(np.stack([a["L0_ffn_shared_in_w"].T.reshape(EMB, 4, EMB), a["L0_ffn_expert_in_w"].T.reshape(EMB, 4, EMB)], 1))
    wso = lay(a["L0_ffn_shared_out_w"].T.reshape(NK, EMB, EMB).transpose(1, 0, 2))
    weo = lay(a["L0_ffn_expert_out_weight"].reshape(EXPERTS, EMB, NK, EMB).transpose(3, 0, 2, 1))
    misc = np.zeros((EMB, MISC), np.float32)
    misc[:, M_GATES:M_GBIAS] = np.concatenate([a["L0_ffn_group_gate_w"], a["L0_ffn_expert_gate_w"]], 0).T
    tri = (np.arange(EG)[None, :] < np.arange(EG)[:, None]).astype(np.float32).reshape(-1)
    misc[0:TOKENS, M_GBIAS:M_EBIAS] = np.concatenate([a["L0_ffn_group_bias"], a["L0_ffn_expert_bias"], tri])
    misc[24:32, M_EBIAS:M_SEL] = a["L0_ffn_expert_out_bias"]
    for e in range(EXPERTS):
        misc[[e, EXPERTS + e, 2 * EXPERTS + e], M_SEL + e] = 1.0

    arrays = dict(cols=cols, eob=eob, patches=patches, wtok=wtok, w3pe=w3pe, stats=stats, wqkvo=wqkvo, win=win, wso=wso,
                  weo=weo, misc=misc)
    nc = bacc.Bacc("TRN2", target_bir_lowering=False, num_devices=1)
    args = [nc.dram_tensor(k, v.shape, F32, kind="ExternalInput").ap() for k, v in arrays.items()]
    out = nc.dram_tensor("out", (EMB, HALVES * HT), F32, kind="ExternalOutput").ap()
    vit_tower(nc, *args, out)
    r = run(nc, [arrays], core_ids=[0])
    return lay(r.results[0]["out"].T.reshape(IMAGES, TOKENS, EMB))
```

```python
from contextlib import ExitStack

import concourse.bass as bass
from concourse import mybir


EMB = 128
IMAGES = 8
PATCHES = 64
TOKENS = PATCHES + 1
PATCH_IN = 256
K_IN = PATCH_IN // EMB
HALVES = 2
HI = IMAGES // HALVES
HP = HI * PATCHES
HT = HI * TOKENS
CHUNKS = 8
DH = EMB // CHUNKS
GROUPS = 8
UG = 2
UNIT = UG * HI
UNITS = GROUPS // UG
HID = 256
NK = HID // EMB
PAIRS = 2 * NK
PAIR_ORDER = (2, 3, 0, 1)
EXPERTS = 8
EGROUPS = 2
EG = EXPERTS // EGROUPS
NG = EGROUPS + EXPERTS
BANK = 512
PART = GROUPS // 2
SCALE = float(DH) ** -0.5
EPS = 1e-5
TOPK_EPS = 1e-8
GATE_CAP = 20.0

(C_EI1, C_EI1B, C_EI2, C_EI2B, C_EO1, C_EO2, C_B1, C_B2, C_SB1, C_SB2, C_B3, C_BQ, C_BK, C_BV, C_BO, C_GAMMA,
 C_BETA, C_LNS, C_LNB, C_SOB, C_CLS) = range(21)
NCOL = 21
NEPS = 6
M_GATES, M_GBIAS = 0, NG
M_EBIAS = M_GBIAS + NG + EG * EG
M_SEL = M_EBIAS + EMB
MISC = M_SEL + EXPERTS

F32 = mybir.dt.float32
BF16 = mybir.dt.bfloat16
ALU = mybir.AluOpType
ACT = mybir.ActivationFunctionType
AX = mybir.AxisListType
ALL_UNITS = HALVES * UNITS
EXP_ZERO = -87.3365
SIG_CAP = 2.0 ** 63
WARM = 5
WARM_REGROUP = 4
WARM_KEYS = 1
WARM_START = (1, 1, 1, 0, 2)
WARM_ROUTE = (3, 1, 1)
WARM_TAIL = (1, 2)
WARM_UNIT = (64, 128)
POOL_EXPERTS = ((2, 5), ())


def vit_tower(nc, cols, eob, patches, wtok, w3pe, stats, wqkvo, win, wso, weo, misc, out):
    with ExitStack() as ctx:
        def sb(name, shape, dt=F32):
            return ctx.enter_context(nc.sbuf_tensor(name, shape, dt))

        def sem(name):
            return ctx.enter_context(nc.semaphore(name))

        cols_s = sb("cols_s", [EMB, NCOL])
        eps_in = sb("eps_in", [EMB, NEPS + 2 * EMB])
        x_s = sb("x_s", [EMB, HALVES, K_IN, HP])
        wtok_s = sb("wtok_s", [EMB, 2, 2, K_IN, EMB])
        w3pe_s = sb("w3pe_s", [EMB, EMB + PATCHES])
        stats_s = sb("stats_s", [EMB, 3, EMB])
        ident, center, mean = stats_s[:, 0, :], stats_s[:, 1, :], stats_s[:, 2, :]
        wqkvo_s = sb("wqkvo_s", [EMB, 4, EMB])
        win_s = sb("win_s", [EMB, 2, 4, EMB])
        wso_s = sb("wso_s", [EMB, NK, EMB])
        weo_s = sb("weo_s", [EMB, EXPERTS, NK, EMB])
        misc_s = sb("misc_s", [EMB, MISC])
        gates_s = misc_s[:, M_GATES:M_GBIAS]
        gbias_s = misc_s[0:TOKENS, M_GBIAS:M_EBIAS]
        ebias_s = misc_s[0:32, M_EBIAS:M_SEL]
        sel_s = misc_s[0:32, M_SEL:MISC]
        selb = sb("selb", [32, EXPERTS, EMB], BF16)

        bias_t = sb("bias_t", [EMB, 3])
        zeros = sb("zeros", [EMB, HP])
        fabs = sb("fabs", [EMB, NEPS + 2 * EMB])
        froot = sb("froot", [EMB, NEPS + 2 * EMB])
        fneg = sb("fneg", [EMB, NEPS + 2 * EMB])
        fsign = sb("fsign", [EMB, NEPS + 2 * EMB])
        fnoise = sb("fnoise", [EMB, NEPS + 2 * EMB])
        sig_eo = sb("sig_eo", [EMB, 2, K_IN, EMB])
        wn = sb("wn", [EMB, 2, K_IN, EMB])
        bn = sb("bn", [EMB, 2])
        gcap = sb("gcap", [EMB, HALVES, HP])
        eg = sb("eg", [EMB, HALVES, HP])
        tnum = sb("tnum", [EMB, HALVES, HP])
        tln = sb("tln", [EMB, HALVES, HP])
        trec = sb("trec", [EMB, HALVES, HP])
        gnum = sb("gnum", [EMB, HALVES, HP])
        inum = sb("inum", [EMB, HALVES, HP])
        prod = sb("prod", [EMB, HALVES, HP])
        X = sb("X", [EMB, HALVES, HI, TOKENS])
        XB = sb("XB", [EMB, HALVES, HT])
        center_gamma = sb("center_gamma", [EMB, EMB])
        sq = sb("sq", [EMB, 3, HALVES, HT])
        lnv = sb("lnv", [EMB, 3, HALVES, HT])
        xc = sb("xc", [EMB, 3, HALVES, HT])
        rstd = sb("rstd", [EMB, 3, HALVES, HT])
        n1 = sb("n1", [EMB, HALVES, HT])
        qkv_f = sb("qkv_f", [EMB, HALVES, HI, 3, TOKENS])
        qkv_c = sb("qkv_c", [EMB, HALVES, CHUNKS, 3, TOKENS])
        q_l = sb("q_l", [EMB, HALVES, TOKENS, CHUNKS])
        v_l = sb("v_l", [EMB, HALVES, TOKENS, CHUNKS])
        k_l = sb("k_l", [EMB, HALVES, HI, TOKENS, CHUNKS])
        v1 = sb("v1", [TOKENS, HALVES, GROUPS, HI, DH + 1])
        mx = sb("mx", [TOKENS, 2, UNIT])
        prob = sb("prob", [TOKENS, 3, UNIT, TOKENS])
        probT = sb("probT", [TOKENS, 2, UNIT, TOKENS])
        rden = sb("rden", [TOKENS, 2, UNIT])
        ctxn = sb("ctxn", [TOKENS, HALVES, GROUPS, HI, 32])
        ctx_c = sb("ctx_c", [EMB, HALVES, CHUNKS, TOKENS])
        ctx_f = sb("ctx_f", [EMB, HALVES, HI, TOKENS])
        y = sb("y", [EMB, HALVES, HT])
        z = sb("z", [EMB, HALVES, HT])
        h2 = sb("h2", [EMB, HALVES, HT])
        zf = sb("zf", [EMB, HALVES, HT])
        flat = sb("flat", [EMB, HALVES, HT])
        ea = sb("ea", [EMB, 2, HT])
        da = sb("da", [EMB, 2, HT])
        la = sb("la", [EMB, 2, HT])
        ra = sb("ra", [EMB, 2, HT])
        sa = sb("sa", [EMB, 2, HT])
        hid = sb("hid", [EMB, HALVES, PAIRS, HT])
        cb_s = sb("cb_s", [EMB, 2, HT])
        hsc = sb("hsc", [EMB, 3, NK, HT])
        hsp = sb("hsp", [EMB, 2, NK, HT])
        o_s = sb("o_s", [EMB, HALVES, HT])
        lg = sb("lg", [TOKENS, HALVES, HI, NG])
        gm = sb("gm", [TOKENS, HALVES, HI, EGROUPS])
        em = sb("em", [TOKENS, HALVES, HI, EGROUPS, EG])
        es = sb("es", [TOKENS, HALVES, HI, EG])
        emax = sb("emax", [TOKENS, HALVES, HI])
        ed = sb("ed", [TOKENS, HALVES, HI, EG])
        ec = sb("ec", [TOKENS, HALVES, HI, EG])
        ee = sb("ee", [TOKENS, HALVES, HI, EG])
        esum = sb("esum", [TOKENS, HALVES, HI])
        gt = sb("gt", [TOKENS, HALVES, HI, EG * EG])
        eq = sb("eq", [TOKENS, HALVES, HI, EG * EG])
        rank = sb("rank", [TOKENS, HALVES, HI, EG])
        top = sb("top", [TOKENS, HALVES, HI, EG])
        ptop = sb("ptop", [TOKENS, HALVES, HI, EG])
        psum_top = sb("psum_top", [TOKENS, HALVES, HI])
        rtop = sb("rtop", [TOKENS, HALVES, HI])
        wtop = sb("wtop", [TOKENS, HALVES, HI, EG])
        comb = sb("comb", [TOKENS, HALVES, HI, EXPERTS])
        rest = sb("rest", [TOKENS, HALVES, HI, EXPERTS])
        route = sb("route", [TOKENS, HALVES, HI, 4, EXPERTS], BF16)
        identb = sb("identb", [EMB, EMB], BF16)
        routeT = sb("routeT", [32, HALVES, HT], BF16)
        routeTf = sb("routeTf", [32, HALVES, HT])

        PS = ctx.enter_context(nc.psum_tensor("PS", [EMB, 8, BANK], F32))

        def bank(b, n=BANK, rows=EMB):
            return PS[0:rows, b, 0:n]

        s_cols, s_eob, s_wtok, s_x = sem("s_cols"), sem("s_eob"), [sem("s_wtok0"), sem("s_wtok1")], [sem("s_x0"), sem("s_x1")]
        s_w3pe, s_stats, s_wqkvo, s_win = sem("s_w3pe"), sem("s_stats"), sem("s_wqkvo"), sem("s_win")
        s_wso, s_weo, s_misc = sem("s_wso"), sem("s_weo"), sem("s_misc")
        s_zero, s_zk, s_ones, s_zctx, s_selb, s_identb, s_eps, s_zeros = (
            sem("s_zero"), sem("s_zk"), sem("s_ones"), sem("s_zctx"), sem("s_selb"), sem("s_identb"), sem("s_eps"), sem("s_zeros"))
        s_fneg = sem("s_fneg")
        s_fabs, s_froot, s_fsign, s_fnoise = sem("s_fabs"), sem("s_froot"), sem("s_fsign"), sem("s_fnoise")
        s_sig, s_wn, s_bn = sem("s_sig"), sem("s_wn"), sem("s_bn")
        s_gate_mm, s_inner_mm, s_gcap, s_eg = sem("s_gate_mm"), sem("s_inner_mm"), sem("s_gcap"), sem("s_eg")
        s_tnum, s_tln, s_trec, s_gnum, s_inum = sem("s_tnum"), sem("s_tln"), sem("s_trec"), sem("s_gnum"), sem("s_inum")
        s_prod, s_tok_mm, s_X, s_cls, s_XB = sem("s_prod"), sem("s_tok_mm"), sem("s_X"), sem("s_cls"), sem("s_XB")
        s_cen = [sem(f"s_cen{i}") for i in range(3)]
        s_sq = [sem(f"s_sq{i}") for i in range(3)]
        s_var = [sem(f"s_var{i}") for i in range(3)]
        s_xc = [sem(f"s_xc{i}") for i in range(3)]
        s_lnv = [sem(f"s_lnv{i}") for i in range(3)]
        s_rstd = [sem(f"s_rstd{i}") for i in range(3)]
        s_n1 = sem("s_n1")
        s_qkv_mm, s_qk, s_v, s_qkvc = sem("s_qkv_mm"), sem("s_qk"), sem("s_v"), [
            [sem(f"s_qkvc{h}_{i}") for i in range(HI)] for h in range(HALVES)]
        s_lq, s_lk, s_lv, s_vT, s_v1 = sem("s_lq"), sem("s_lk"), sem("s_lv"), sem("s_vT"), sem("s_v1")
        s_lkd = sem("s_lkd")
        s_score, s_mx, s_sub, s_exp, s_pT, s_pTs, s_pv, s_rden, s_ctxn = (
            sem("s_score"), sem("s_mx"), sem("s_sub"), sem("s_exp"), sem("s_pT"), sem("s_pTs"), sem("s_pv"),
            sem("s_rden"), sem("s_ctxn"))
        s_ctxT, s_ctxc, s_ctxf = sem("s_ctxT"), sem("s_ctxc"), [sem("s_ctxf0"), sem("s_ctxf1")]
        s_o_mm, s_y, s_z, s_h2, s_zf, s_flat = sem("s_o_mm"), sem("s_y"), sem("s_z"), sem("s_h2"), sem("s_zf"), sem("s_flat")
        s_cgamma = sem("s_cgamma")
        s_wtop, s_part = sem("s_wtop"), [sem("s_part0"), sem("s_part1")]
        s_lg_mm, s_route_step, s_ed, s_ee, s_route, s_routeT_mm, s_routeT, s_routeTf = (
            sem("s_lg_mm"), sem("s_route_step"), sem("s_ed"), sem("s_ee"), [sem("s_route0"), sem("s_route1")], sem("s_routeT_mm"),
            sem("s_routeT"), sem("s_routeTf"))
        s_ab, s_ea, s_da, s_la, s_ra, s_sa, s_hid = (
            sem("s_ab"), sem("s_ea"), sem("s_da"), sem("s_la"), sem("s_ra"), sem("s_sa"), sem("s_hid"))
        s_cb, s_cbs, s_hsc, s_hsp, s_ehid = sem("s_cb"), sem("s_cbs"), sem("s_hsc"), sem("s_hsp"), sem("s_ehid")
        s_o, s_out = sem("s_o"), sem("s_out")

        def gate_bank(h, net):
            return 2 * h + net

        def tok_bank(h):
            return 4 + h

        def cen_bank(h):
            return 6 + h

        def qkv_bank(h, c):
            return (2 * h, 2 * h + 1, 4 + h)[c]

        NORM_BANK = 7

        def scores(n):
            b = UG * (n % 2)
            return PS[0:TOKENS, b:b + UG, 0:HT].rearrange("p g (i k) -> p g i k", k=TOKENS)

        probTs = PS[0:TOKENS, 4:4 + UG, 0:HT].rearrange("p g (i k) -> p g i k", k=TOKENS)
        pv = PS[0:TOKENS, 6, 0:UNIT * 32].rearrange("p (g d) -> p g d", d=32)

        def vT(h, part):
            return PS[0:TOKENS, (4 + part, NORM_BANK)[h]].rearrange("p (g c) -> p g c", c=EMB)

        def ctxT(h, part):
            return bank((4 + part, NORM_BANK)[1 - h], PART * TOKENS)

        PAIR_SLOTS = (0, 1, 2, 0, 1, 0, 1, 0)

        def pair_banks(n):
            return (2 * PAIR_SLOTS[n], 2 * PAIR_SLOTS[n] + 1)

        def cb_bank(e):
            return 4 + e % 2

        def y_bank(h):
            return 6 + h

        def routeT_p(h):
            return PS[0:32, (3, NORM_BANK)[h], 0:HI * 33].bitcast(BF16).rearrange("p (i t) -> p i t", i=HI)[:, :, 0:TOKENS]

        def logits(h):
            return PS[0:TOKENS, NORM_BANK, 0:HI * 16].rearrange("p (i n) -> p i n", i=HI)[:, :, 0:NG]

        def dve_experts(h, e):
            return len([i for i in range(EXPERTS * h + e + 1) if i % EXPERTS not in POOL_EXPERTS[i // EXPERTS]])

        def pool_experts(h, e):
            return len([i for i in range(EXPERTS * h + e + 1) if i % EXPERTS in POOL_EXPERTS[i // EXPERTS]])

        def regrouped(eng, h):
            for i in range(HI):
                eng.wait_ge(s_qkvc[h][i], 16)

        def keys_of(eng, h, i, copy, done):
            rows = slice(32 * i, 32 * i + 32)
            eng.wait_ge(s_qkvc[h][i], 16)
            copy(k_l[rows, h, i].rearrange("p t j -> p j t"), qkv_c[rows, h, :, 1]).then_inc(done, 1)

        def per_image(t, h):
            return t[:, h].unsqueeze(2).to_broadcast([TOKENS, HI, EG])

        def group_mask(h):
            return gm[:, h].unsqueeze(3).to_broadcast([TOKENS, HI, EGROUPS, EG])

        def both_groups(t, h):
            return t[:, h].unsqueeze(2).to_broadcast([TOKENS, HI, EGROUPS, EG])

        ROUTE_STEPS = 13
        SQUARE = "p i (e j) -> p i e j"
        BY_GROUP = "p i (g e) -> p i g e"

        block = ctx.enter_context(nc.Block())

        @block.sync
        def _(sp):
            sp.dma_start(eps_in[:, 0:NEPS], cols[:, 0:NEPS]).then_inc(s_eob, 16)
            sp.dma_start(eps_in[:, NEPS:NEPS + 2 * EMB], eob.partition_broadcast(EMB)).then_inc(s_eob, 16)
            for net in range(2):
                sp.dma_start(wtok_s[:, net], wtok[:, net]).then_inc(s_wtok[net], 16)
            sp.dma_start(x_s[:, 0], patches[0]).then_inc(s_x[0], 16)
            sp.dma_start(cols_s[:], cols).then_inc(s_cols, 16)
            sp.dma_start(x_s[:, 1], patches[1]).then_inc(s_x[1], 16)
            sp.dma_start(w3pe_s[:], w3pe).then_inc(s_w3pe, 16)
            sp.dma_start(stats_s[:], stats).then_inc(s_stats, 16)
            sp.dma_start(wqkvo_s[:], wqkvo).then_inc(s_wqkvo, 16)
            sp.dma_start(misc_s[:], misc).then_inc(s_misc, 16)
            sp.dma_start(win_s[:], win).then_inc(s_win, 16)
            sp.dma_start(wso_s[:], wso).then_inc(s_wso, 16)
            sp.dma_start(weo_s[:], weo).then_inc(s_weo, 16)
            for h in range(HALVES):
                sp.wait_ge(s_qk, 2 * (h + 1))
                sp.wait_ge(s_v, h + 1)
                sp.wait_ge(s_zero, 1)
                for i in range(HI):
                    sp.dma_start(qkv_c[32 * i:32 * i + DH, h].rearrange("d j c t -> d j (c t)"),
                                 qkv_f[:, h, i].rearrange("p c t -> p (c t)")).then_inc(s_qkvc[h][i], 16)
            for h in range(HALVES):
                sp.wait_ge(s_ctxc, 2 * (h + 1))
                for i in range(HI):
                    sp.dma_start(ctx_f[:, h, i, :], ctx_c[32 * i:32 * i + DH, h]).then_inc(s_ctxf[h], 16)
            for h in range(HALVES):
                sp.wait_ge(s_o, h + 1)
                sp.dma_start(out[:, h * HT:(h + 1) * HT], o_s[:, h]).then_inc(s_out, 16)
            sp.wait_ge(s_out, 16 * HALVES)

        @block.gpsimd
        def _(pool):
            nc.gpsimd.memset(qkv_c[:], 0.0).then_inc(s_zero, 1)
            nc.gpsimd.memset(k_l[:, 0], 0.0).then_inc(s_zk, 1)
            nc.gpsimd.memset(v1[:], 1.0).then_inc(s_ones, 1)
            nc.gpsimd.memset(ctxn[:], 0.0).then_inc(s_zctx, 1)
            nc.gpsimd.memset(k_l[:, 1], 0.0).then_inc(s_zk, 1)
            pool.wait_ge(s_misc, 16)
            nc.gpsimd.tensor_copy(selb[:], sel_s.unsqueeze(2).to_broadcast([32, EXPERTS, EMB])).then_inc(s_selb, 1)
            pool.wait_ge(s_stats, 16)
            nc.gpsimd.tensor_copy(identb[:], ident).then_inc(s_identb, 1)
            pool.wait_ge(s_cols, 16)
            nc.gpsimd.tensor_scalar(center_gamma[:], center, cols_s[:, C_GAMMA:C_GAMMA + 1], None,
                                    ALU.mult).then_inc(s_cgamma, 1)
            for h in range(HALVES):
                pool.wait_ge(s_X, h + 1)
                pool.wait_ge(s_cls, 1)
                nc.gpsimd.tensor_scalar(XB[:, h], X[:, h].rearrange("p i t -> p (i t)"),
                                        cols_s[:, C_BETA:C_BETA + 1], None, ALU.add).then_inc(s_XB, 1)
            for h in range(HALVES):
                regrouped(pool, h)
                nc.gpsimd.tensor_copy(v_l[:, h].rearrange("p t j -> p j t"), qkv_c[:, h, :, 2]).then_inc(s_lv, 1)

            def expert_hidden(h, e):
                n = pool_experts(h, e)
                pool.wait_ge(s_cbs, n)
                pool.wait_ge(s_hid, h * PAIRS + NK)
                if n > 2:
                    hb, eb = [(hh, i) for hh in range(HALVES) for i in POOL_EXPERTS[hh]][n - 3]
                    pool.wait_ge(s_ehid, hb * EXPERTS + eb + 1)
                nc.gpsimd.tensor_tensor(hsp[:, n % 2], hid[:, h, NK:PAIRS],
                                        cb_s[:, n % 2].unsqueeze(1).to_broadcast([EMB, NK, HT]),
                                        ALU.mult).then_inc(s_hsp, 1)

            for e in POOL_EXPERTS[0]:
                expert_hidden(0, e)

        @block.scalar
        def _(act):
            nc.scalar.preload_act_table_set("sqrt_and_others")
            act.wait_ge(s_eob, 32)
            nc.scalar.activation(fabs[:], eps_in[:], ACT.Abs).then_inc(s_fabs, 1)
            act.wait_ge(s_fabs, 1)
            nc.scalar.activation(froot[:], fabs[:], ACT.Sqrt).then_inc(s_froot, 1)
            nc.scalar.preload_act_table_set("natural_log_exp_and_others")
            act.wait_ge(s_eps, 3)
            for h in range(HALVES):
                act.wait_ge(s_gcap, h + 1)
                nc.scalar.activation(eg[:, h], gcap[:, h], ACT.Exp).then_inc(s_eg, 1)
                act.wait_ge(s_tnum, h + 1)
                nc.scalar.activation(tln[:, h], tnum[:, h], ACT.Ln, bias=bias_t[:, 2:3]).then_inc(s_tln, 1)
                act.wait_ge(s_tln, h + 1)
                nc.scalar.activation(trec[:, h], tln[:, h], ACT.Exp, scale=-1.0).then_inc(s_trec, 1)

            def norm_square(use, h, b):
                act.wait_ge(s_cen[use], h + 1)
                nc.scalar.activation(sq[:, use, h], bank(b, HT), ACT.Square).then_inc(s_sq[use], 1)
                nc.scalar.copy(xc[:, use, h], bank(b, HT)).then_inc(s_xc[use], 1)

            def norm_rstd(use, h, b, scale=1.0):
                act.wait_ge(s_var[use], h + 1)
                nc.scalar.activation(lnv[:, use, h], bank(b, HT), ACT.Ln, scale=scale,
                                     bias=bias_t[:, int(use == 2):int(use == 2) + 1]).then_inc(s_lnv[use], 1)
                act.wait_ge(s_lnv[use], h + 1)
                nc.scalar.activation(rstd[:, use, h], lnv[:, use, h], ACT.Exp, scale=-0.5).then_inc(s_rstd[use], 1)

            def qk_out(h):
                for c, col in ((0, C_BQ), (1, C_BK)):
                    act.wait_ge(s_qkv_mm, 3 * h + c + 1)
                    nc.scalar.activation(qkv_f[:, h, :, c], bank(qkv_bank(h, c), HT).rearrange("p (i t) -> p i t", i=HI),
                                         ACT.Identity, bias=cols_s[:, col:col + 1]).then_inc(s_qk, 1)

            norm_square(0, 0, cen_bank(0))
            norm_rstd(0, 0, tok_bank(0))
            norm_square(0, 1, cen_bank(1))
            qk_out(0)
            norm_rstd(0, 1, tok_bank(1))
            qk_out(1)

            def values(h, part):
                act.wait_ge(s_vT, 2 * h + part + 1)
                act.wait_ge(s_ones, 1)
                nc.scalar.copy(v1[:, h, part * PART:(part + 1) * PART, :, 0:DH],
                               vT(h, part).rearrange("p g (i d) -> p g i d", d=32)[:, :, :, 0:DH]).then_inc(s_v1, 1)

            def context_out(h, part):
                act.wait_ge(s_ctxT, 2 * h + part + 1)
                src = ctxT(h, part)
                t_mid, j_mid = PART * TOKENS // CHUNKS, PART * TOKENS % CHUNKS
                if part == 0:
                    nc.scalar.copy(ctx_c[:, h, 0:j_mid, t_mid], src[:, t_mid * CHUNKS:PART * TOKENS])
                    whole, tokens = src[:, 0:t_mid * CHUNKS], slice(0, t_mid)
                else:
                    nc.scalar.copy(ctx_c[:, h, j_mid:CHUNKS, t_mid], src[:, 0:CHUNKS - j_mid])
                    whole, tokens = src[:, CHUNKS - j_mid:PART * TOKENS], slice(t_mid + 1, TOKENS)
                nc.scalar.copy(ctx_c[:, h, :, tokens].rearrange("p j t -> p t j"),
                               whole.rearrange("p (t j) -> p t j", j=CHUNKS)).then_inc(s_ctxc, 1)

            def unit_exp(n):
                act.wait_ge(s_sub, n + 1)
                nc.scalar.activation(prob[:, n % 3], prob[:, n % 3], ACT.Exp, scale=SCALE).then_inc(s_exp, 1)

            act.wait_ge(s_zk, 1)
            for i in (0, 1, 3):
                keys_of(act, 0, i, nc.scalar.copy, s_lk)
            unit_exp(0)
            values(0, 0)
            values(0, 1)
            unit_exp(1)
            for n in range(ALL_UNITS):
                act.wait_ge(s_pT, n + 1)
                if n >= 2:
                    act.wait_ge(s_pv, n - 1)
                nc.scalar.copy(probT[:, n % 2].rearrange("p (g i) k -> p g i k", g=UG), probTs).then_inc(s_pTs, 1)
                if n == 0:
                    act.wait_ge(s_zk, 2)
                    keys_of(act, 1, 0, nc.scalar.copy, s_lk)
                if n == 1:
                    keys_of(act, 1, 1, nc.scalar.copy, s_lk)
                if n == 2:
                    values(1, 1)
                if n == 6:
                    norm_square(1, 0, NORM_BANK)
                if n == 4:
                    context_out(0, 1)
                if n + 2 < ALL_UNITS:
                    unit_exp(n + 2)
                if n == 1:
                    values(1, 0)
                if n == 3:
                    context_out(0, 0)
            norm_rstd(1, 0, NORM_BANK)
            context_out(1, 0)
            norm_square(2, 0, NORM_BANK)
            context_out(1, 1)

            def pair_sigmoid(h, q):
                n = h * PAIRS + q
                act.wait_ge(s_da, n + 1)
                nc.scalar.activation(la[:, n % 2], da[:, n % 2], ACT.Ln).then_inc(s_la, 1)
                act.wait_ge(s_la, n + 1)
                if n >= 2:
                    act.wait_ge(s_sa, n - 1)
                nc.scalar.activation(ra[:, n % 2], la[:, n % 2], ACT.Exp, scale=-1.0).then_inc(s_ra, 1)

            def pair_exp(h, q):
                n = h * PAIRS + q
                act.wait_ge(s_ab, n + 1)
                if n >= 2:
                    act.wait_ge(s_da, n - 1)
                nc.scalar.activation(ea[:, n % 2], bank(pair_banks(n)[0], HT), ACT.Exp, scale=-1.0).then_inc(s_ea, 1)

            def router_exp(h):
                act.wait_ge(s_ed, h + 1)
                nc.scalar.activation(ee[:, h], ed[:, h], ACT.Exp).then_inc(s_ee, 1)

            def route_out(h):
                act.wait_ge(s_routeT_mm, h + 1)
                for t, done in ((routeT, s_routeT), (routeTf, s_routeTf)):
                    nc.scalar.copy(t[:, h].rearrange("p (i t) -> p i t", i=HI), routeT_p(h)).then_inc(done, 1)

            def broadcast_out(h, e):
                n = pool_experts(h, e)
                act.wait_ge(s_cb, h * EXPERTS + e + 1)
                if n > 2:
                    act.wait_ge(s_hsp, n - 2)
                nc.scalar.copy(cb_s[:, n % 2], bank(cb_bank(e), HT)).then_inc(s_cbs, 1)

            norm_rstd(2, 0, NORM_BANK, 1.0 + EPS)
            pair_exp(0, 0)
            pair_exp(0, 1)
            router_exp(0)
            pair_sigmoid(0, 0)
            pair_sigmoid(0, 1)
            pair_exp(0, 2)
            pair_exp(0, 3)
            pair_sigmoid(0, 2)
            route_out(0)
            norm_square(1, 1, NORM_BANK)
            norm_rstd(1, 1, NORM_BANK)
            pair_sigmoid(0, 3)
            broadcast_out(0, POOL_EXPERTS[0][0])
            norm_square(2, 1, NORM_BANK)
            norm_rstd(2, 1, NORM_BANK, 1.0 + EPS)
            broadcast_out(0, POOL_EXPERTS[0][1])
            pair_exp(1, 0)
            router_exp(1)
            pair_exp(1, 1)
            pair_sigmoid(1, 0)
            pair_sigmoid(1, 1)
            pair_exp(1, 2)
            route_out(1)
            pair_sigmoid(1, 2)
            pair_exp(1, 3)
            pair_sigmoid(1, 3)

        @block.vector
        def _(dve):
            step = [0]

            def routed(ins):
                step[0] += 1
                ins.then_inc(s_route_step, 1)

            def last_step():
                dve.wait_ge(s_route_step, step[0])

            nc.vector.memset(zeros[:], 0.0).then_inc(s_zeros, 1)
            nc.vector.memset(bias_t[:, 0:1], EPS).then_inc(s_eps, 1)
            nc.vector.memset(bias_t[:, 1:2], EPS * EPS).then_inc(s_eps, 1)
            nc.vector.memset(bias_t[:, 2:3], 2.0).then_inc(s_eps, 1)
            dve.wait_ge(s_eob, 32)
            nc.vector.tensor_single_scalar(fneg[:], eps_in[:], 0.0, ALU.is_lt).then_inc(s_fneg, 1)
            dve.wait_ge(s_fneg, 1)
            nc.vector.scalar_tensor_tensor(out=fsign[:], in0=eps_in[:], scalar=0.0, in1=fneg[:], op0=ALU.is_gt,
                                           op1=ALU.subtract).then_inc(s_fsign, 1)
            dve.wait_ge(s_froot, 1)
            dve.wait_ge(s_fsign, 1)
            nc.vector.tensor_tensor(fnoise[:], froot[:], fsign[:], ALU.mult).then_inc(s_fnoise, 1)
            dve.wait_ge(s_fnoise, 1)
            for net in range(2):
                dve.wait_ge(s_wtok[net], 16)
                nc.vector.tensor_tensor(sig_eo[:, net], wtok_s[:, net, 1],
                                        fnoise[:, NEPS + net * EMB:NEPS + (net + 1) * EMB].unsqueeze(1)
                                        .to_broadcast([EMB, K_IN, EMB]), ALU.mult).then_inc(s_sig, 1)
                dve.wait_ge(s_sig, net + 1)
                for k in range(K_IN):
                    c = 2 * net + k
                    nc.vector.scalar_tensor_tensor(out=wn[:, net, k], in0=sig_eo[:, net, k],
                                                   scalar=fnoise[:, c:c + 1], in1=wtok_s[:, net, 0, k],
                                                   op0=ALU.mult, op1=ALU.add).then_inc(s_wn, 1)
            dve.wait_ge(s_cols, 16)
            for net in range(2):
                nc.vector.scalar_tensor_tensor(out=bn[:, net:net + 1], in0=cols_s[:, C_SB1 + net:C_SB1 + net + 1],
                                               scalar=fnoise[:, C_EO1 + net:C_EO1 + net + 1],
                                               in1=cols_s[:, C_B1 + net:C_B1 + net + 1],
                                               op0=ALU.mult, op1=ALU.add).then_inc(s_bn, 1)
            nc.vector.tensor_copy(X[:, :, :, 0:1], cols_s[:, C_CLS:C_CLS + 1].unsqueeze(1).unsqueeze(1)
                                  .to_broadcast([EMB, HALVES, HI, 1])).then_inc(s_cls, 1)
            dve.wait_ge(s_bn, 2)
            def gate_cap(h):
                dve.wait_ge(s_gate_mm, h + 1)
                nc.vector.tensor_scalar(gcap[:, h], bank(gate_bank(h, 0), HP), bn[:, 0:1], GATE_CAP, ALU.add,
                                        ALU.min).then_inc(s_gcap, 1)

            def gate_start(h):
                dve.wait_ge(s_eg, h + 1)
                nc.vector.scalar_tensor_tensor(out=tnum[:, h], in0=eg[:, h], scalar=2.0, in1=eg[:, h],
                                               op0=ALU.add, op1=ALU.mult).then_inc(s_tnum, 1)

            def gate_numerator(h):
                dve.wait_ge(s_tnum, h + 1)
                nc.vector.scalar_tensor_tensor(out=gnum[:, h], in0=bank(gate_bank(h, 0), HP), scalar=bn[:, 0:1],
                                               in1=tnum[:, h], op0=ALU.add, op1=ALU.mult).then_inc(s_gnum, 1)

            def gate_product(h):
                dve.wait_ge(s_inner_mm, h + 1)
                dve.wait_ge(s_gnum, h + 1)
                nc.vector.scalar_tensor_tensor(out=inum[:, h], in0=bank(gate_bank(h, 1), HP), scalar=bn[:, 1:2],
                                               in1=gnum[:, h], op0=ALU.add, op1=ALU.mult).then_inc(s_inum, 1)
                dve.wait_ge(s_trec, h + 1)
                dve.wait_ge(s_inum, h + 1)
                nc.vector.tensor_tensor(prod[:, h], inum[:, h], trec[:, h], ALU.mult).then_inc(s_prod, 1)

            def tokens(h):
                dve.wait_ge(s_tok_mm, h + 1)
                nc.vector.scalar_tensor_tensor(
                    out=X[:, h, :, 1:TOKENS], in0=bank(tok_bank(h), HP).rearrange("p (i t) -> p i t", i=HI),
                    scalar=cols_s[:, C_B3:C_B3 + 1],
                    in1=w3pe_s[:, EMB:EMB + PATCHES].unsqueeze(1).to_broadcast([EMB, HI, PATCHES]),
                    op0=ALU.add, op1=ALU.add).then_inc(s_X, 1)

            def norm_rows(h):
                dve.wait_ge(s_rstd[0], h + 1)
                dve.wait_ge(s_xc[0], h + 1)
                nc.vector.tensor_tensor(n1[:, h], xc[:, 0, h], rstd[:, 0, h], ALU.mult).then_inc(s_n1, 1)

            def value_out(h):
                dve.wait_ge(s_qkv_mm, 3 * h + 3)
                nc.vector.tensor_scalar(qkv_f[:, h, :, 2], bank(qkv_bank(h, 2), HT).rearrange("p (i t) -> p i t", i=HI),
                                        cols_s[:, C_BV:C_BV + 1], None, ALU.add).then_inc(s_v, 1)

            gate_cap(0)
            gate_start(0)
            gate_numerator(0)
            gate_cap(1)
            gate_product(0)
            gate_start(1)
            dve.wait_ge(s_w3pe, 16)
            tokens(0)
            gate_numerator(1)
            gate_product(1)
            tokens(1)
            norm_rows(0)
            value_out(0)
            norm_rows(1)
            value_out(1)

            def queries(h):
                regrouped(dve, h)
                nc.vector.tensor_copy(q_l[:, h].rearrange("p t j -> p j t"), qkv_c[:, h, :, 0]).then_inc(s_lq, 1)

            dve.wait_ge(s_zk, 1)
            keys_of(dve, 0, 2, nc.vector.tensor_copy, s_lkd)
            queries(0)

            def softmax_shift(n):
                dve.wait_ge(s_score, n + 1)
                nc.vector.tensor_reduce(mx[:, n % 2].rearrange("p (g i) -> p g i", g=UG), scores(n), AX.X,
                                        ALU.max).then_inc(s_mx, 1)
                dve.wait_ge(s_mx, n + 1)
                if n >= 3:
                    dve.wait_ge(s_pT, n - 2)
                nc.vector.tensor_tensor(prob[:, n % 3].rearrange("p (g i) k -> p g i k", g=UG), scores(n),
                                        mx[:, n % 2].rearrange("p (g i) -> p g i", g=UG).unsqueeze(3)
                                        .to_broadcast([TOKENS, UG, HI, TOKENS]), ALU.subtract).then_inc(s_sub, 1)

            def context_norm(n):
                h, u = n // UNITS, n % UNITS
                dve.wait_ge(s_pv, n + 1)
                nc.vector.reciprocal(rden[:, n % 2], pv[:, :, DH]).then_inc(s_rden, 1)
                dve.wait_ge(s_rden, n + 1)
                nc.vector.tensor_tensor(
                    ctxn[:, h, UG * u:UG * u + UG, :, 0:DH],
                    pv[:, :, 0:DH].rearrange("p (g i) d -> p g i d", g=UG),
                    rden[:, n % 2].rearrange("p (g i) -> p g i", g=UG).unsqueeze(3)
                    .to_broadcast([TOKENS, UG, HI, DH]), ALU.mult).then_inc(s_ctxn, 1)

            def residual(h):
                dve.wait_ge(s_o_mm, h + 1)
                nc.vector.scalar_tensor_tensor(out=y[:, h], in0=bank(NORM_BANK, HT), scalar=cols_s[:, C_BO:C_BO + 1],
                                               in1=n1[:, h], op0=ALU.add, op1=ALU.add).then_inc(s_y, 1)

            def attended_rows(h):
                dve.wait_ge(s_rstd[1], h + 1)
                dve.wait_ge(s_xc[1], h + 1)
                nc.vector.tensor_tensor(z[:, h], xc[:, 1, h], rstd[:, 1, h], ALU.mult).then_inc(s_z, 1)

            def hidden_rows(h):
                dve.wait_ge(s_z, h + 1)
                dve.wait_ge(s_XB, h + 1)
                nc.vector.scalar_tensor_tensor(out=h2[:, h], in0=z[:, h], scalar=cols_s[:, C_GAMMA:C_GAMMA + 1],
                                               in1=XB[:, h], op0=ALU.mult, op1=ALU.add).then_inc(s_h2, 1)

            def flat_rows(h):
                dve.wait_ge(s_rstd[2], h + 1)
                dve.wait_ge(s_xc[2], h + 1)
                nc.vector.tensor_tensor(zf[:, h], xc[:, 2, h], rstd[:, 2, h], ALU.mult).then_inc(s_zf, 1)
                dve.wait_ge(s_zf, h + 1)
                nc.vector.tensor_scalar(flat[:, h], zf[:, h], cols_s[:, C_LNS:C_LNS + 1],
                                        cols_s[:, C_LNB:C_LNB + 1], ALU.mult, ALU.add).then_inc(s_flat, 1)

            def router_logits(h):
                dve.wait_ge(s_lg_mm, h + 1)
                routed(nc.vector.tensor_tensor(
                    lg[:, h], logits(h),
                    gbias_s[:, 0:NG].unsqueeze(1).to_broadcast([TOKENS, HI, NG]), ALU.add))
                last_step()
                nc.vector.tensor_tensor(gm[:, h, :, 0:1], lg[:, h, :, 0:1], lg[:, h, :, 1:2], ALU.is_ge)
                routed(nc.vector.tensor_tensor(gm[:, h, :, 1:2], lg[:, h, :, 0:1], lg[:, h, :, 1:2], ALU.is_lt))

            def router_group(h):
                last_step()
                routed(nc.vector.tensor_tensor(em[:, h], lg[:, h, :, EGROUPS:NG].rearrange("p i (g e) -> p i g e", e=EG),
                                               group_mask(h), ALU.mult))
                last_step()
                routed(nc.vector.tensor_tensor(es[:, h], em[:, h, :, 0], em[:, h, :, 1], ALU.add))

            def router_shift(h):
                last_step()
                routed(nc.vector.tensor_reduce(emax[:, h], es[:, h], AX.X, ALU.max))
                last_step()
                nc.vector.tensor_tensor(ed[:, h], es[:, h], per_image(emax, h), ALU.subtract).then_inc(s_ed, 1)
                dve.wait_ge(s_ed, h + 1)
                routed(nc.vector.tensor_single_scalar(ec[:, h], ed[:, h], EXP_ZERO, ALU.max))

            def router_compare(h):
                last_step()
                l_j = ec[:, h].unsqueeze(2).to_broadcast([TOKENS, HI, EG, EG])
                l_e = ec[:, h].unsqueeze(3).to_broadcast([TOKENS, HI, EG, EG])
                nc.vector.tensor_tensor(gt[:, h].rearrange(SQUARE, e=EG), l_j, l_e, ALU.is_gt)
                routed(nc.vector.tensor_tensor(eq[:, h].rearrange(SQUARE, e=EG), l_j, l_e, ALU.is_equal))

            def router_ties(h):
                last_step()
                routed(nc.vector.tensor_tensor(eq[:, h], eq[:, h],
                                               gbias_s[:, NG:NG + EG * EG].unsqueeze(1)
                                               .to_broadcast([TOKENS, HI, EG * EG]), ALU.mult))
                last_step()
                routed(nc.vector.tensor_tensor(gt[:, h], gt[:, h], eq[:, h], ALU.add))

            def router_rank(h):
                last_step()
                routed(nc.vector.tensor_reduce(rank[:, h], gt[:, h].rearrange(SQUARE, e=EG), AX.X, ALU.add))

            def router_top(h):
                last_step()
                dve.wait_ge(s_ee, h + 1)
                nc.vector.tensor_reduce(esum[:, h], ee[:, h], AX.X, ALU.add)
                nc.vector.tensor_single_scalar(top[:, h], rank[:, h], 1.5, ALU.is_lt)
                routed(nc.vector.scalar_tensor_tensor(out=ptop[:, h], in0=rank[:, h], scalar=1.5, in1=ee[:, h],
                                                      op0=ALU.is_lt, op1=ALU.mult))

            def router_norm(h):
                last_step()
                routed(nc.vector.tensor_reduce(psum_top[:, h], ptop[:, h], AX.X, ALU.add))
                last_step()
                routed(nc.vector.scalar_tensor_tensor(out=psum_top[:, h], in0=esum[:, h], scalar=TOPK_EPS,
                                                      in1=psum_top[:, h], op0=ALU.mult, op1=ALU.add))

            def router_weights(h):
                last_step()
                routed(nc.vector.reciprocal(rtop[:, h], psum_top[:, h]))
                last_step()
                nc.vector.tensor_tensor(wtop[:, h], ptop[:, h], per_image(rtop, h), ALU.mult).then_inc(s_wtop, 1)

            def route_columns(h):
                nc.vector.tensor_tensor(comb[:, h].rearrange(BY_GROUP, e=EG), both_groups(wtop, h), group_mask(h),
                                  ALU.mult).then_inc(s_part[h], 1)

            def route_part0(h):
                dve.wait_ge(s_part[h], 1)
                nc.vector.tensor_copy(route[:, h, :, 0], comb[:, h]).then_inc(s_part[h], 1)
                dve.wait_ge(s_part[h], 2)
                nc.vector.tensor_tensor(rest[:, h], comb[:, h], route[:, h, :, 0], ALU.subtract).then_inc(s_part[h], 1)

            def route_part1(h):
                dve.wait_ge(s_part[h], 3)
                nc.vector.tensor_copy(route[:, h, :, 1], rest[:, h]).then_inc(s_part[h], 1)

            def route_rest(h):
                nc.vector.tensor_tensor(route[:, h, :, 3].rearrange(BY_GROUP, e=EG), both_groups(top, h), group_mask(h),
                                  ALU.mult).then_inc(s_route[h], 1)
                dve.wait_ge(s_part[h], 4)
                nc.vector.tensor_tensor(route[:, h, :, 2], rest[:, h], route[:, h, :, 1],
                                        ALU.subtract).then_inc(s_route[h], 1)

            def sigmoid_sum(n):
                dve.wait_ge(s_ea, n + 1)
                if n >= 2:
                    dve.wait_ge(s_la, n - 1)
                nc.vector.tensor_scalar(da[:, n % 2], ea[:, n % 2], SIG_CAP, 1.0, ALU.min,
                                        ALU.add).then_inc(s_da, 1)

            def swiglu_in(n):
                a = bank(pair_banks(n)[0], HT)
                dve.wait_ge(s_ra, n + 1)
                nc.vector.tensor_tensor(sa[:, n % 2], a, ra[:, n % 2], ALU.mult).then_inc(s_sa, 1)

            def swiglu_out(n):
                h, q = n // PAIRS, PAIR_ORDER[n % PAIRS]
                b = bank(pair_banks(n)[1], HT)
                dve.wait_ge(s_sa, n + 1)
                nc.vector.tensor_tensor(hid[:, h, q], b, sa[:, n % 2], ALU.mult).then_inc(s_hid, 1)

            def swiglu(n):
                swiglu_in(n)
                swiglu_out(n)

            def expert_hidden(h, e):
                if e in POOL_EXPERTS[h]:
                    return
                n = dve_experts(h, e)
                dve.wait_ge(s_hid, h * PAIRS + NK)
                dve.wait_ge(s_cb, h * EXPERTS + e + 1)
                if n > 3:
                    hb, eb = [(hh, i) for hh in range(HALVES) for i in range(EXPERTS) if i not in POOL_EXPERTS[hh]][n - 4]
                    dve.wait_ge(s_ehid, hb * EXPERTS + eb + 1)
                nc.vector.tensor_tensor(hsc[:, n % 3], hid[:, h, NK:PAIRS],
                                        bank(cb_bank(e), HT).unsqueeze(1).to_broadcast([EMB, NK, HT]),
                                        ALU.mult).then_inc(s_hsc, 1)

            def result(h):
                dve.wait_ge(s_ehid, (h + 1) * EXPERTS)
                nc.vector.scalar_tensor_tensor(out=o_s[:, h], in0=bank(y_bank(h), HT), scalar=cols_s[:, C_SOB:C_SOB + 1],
                                               in1=h2[:, h], op0=ALU.add, op1=ALU.add).then_inc(s_o, 1)

            dve.wait_ge(s_zctx, 1)
            softmax_shift(0)
            softmax_shift(1)
            for n in range(ALL_UNITS):
                if n + 2 < ALL_UNITS:
                    softmax_shift(n + 2)
                if n == 6:
                    residual(0)
                if n == 7:
                    attended_rows(0)
                context_norm(n)
                if n == 0:
                    queries(1)
                    dve.wait_ge(s_zk, 2)
                    keys_of(dve, 1, 2, nc.vector.tensor_copy, s_lkd)
                if n == 1:
                    keys_of(dve, 1, 3, nc.vector.tensor_copy, s_lkd)
            hidden_rows(0)
            flat_rows(0)
            router_logits(0)
            router_group(0)
            router_shift(0)
            router_compare(0)
            sigmoid_sum(0)
            router_ties(0)
            sigmoid_sum(1)
            router_rank(0)
            router_top(0)
            swiglu_in(0)
            router_norm(0)
            swiglu_out(0)
            router_weights(0)
            swiglu_in(1)
            swiglu_out(1)
            dve.wait_ge(s_wtop, 1)
            route_columns(0)
            sigmoid_sum(2)
            route_part0(0)
            residual(1)
            route_part1(0)
            route_rest(0)
            swiglu(2)
            sigmoid_sum(3)
            expert_hidden(0, 0)
            expert_hidden(0, 1)
            attended_rows(1)
            hidden_rows(1)
            swiglu(3)
            expert_hidden(0, 3)
            expert_hidden(0, 4)
            flat_rows(1)
            router_logits(1)
            router_group(1)
            router_shift(1)
            router_compare(1)
            sigmoid_sum(4)
            router_ties(1)
            router_rank(1)
            expert_hidden(0, 6)
            router_top(1)
            sigmoid_sum(5)
            router_norm(1)
            swiglu_in(4)
            swiglu_out(4)
            router_weights(1)
            dve.wait_ge(s_wtop, 2)
            route_columns(1)
            expert_hidden(0, 7)
            route_part0(1)
            route_part1(1)
            route_rest(1)
            swiglu(5)
            sigmoid_sum(6)
            expert_hidden(1, 0)
            expert_hidden(1, 1)
            sigmoid_sum(7)
            expert_hidden(1, 2)
            swiglu(6)
            swiglu(7)
            expert_hidden(1, 3)
            result(0)
            for e in range(4, EXPERTS):
                expert_hidden(1, e)
            result(1)

        @block.tensor
        def _(pe):
            mm = nc.tensor.matmul
            pe.wait_ge(s_zeros, 1)

            def keep_warm(count, b=NORM_BANK, n=HP):
                for _w in range(count):
                    mm(bank(b, n), zeros[:, 0:EMB], zeros[:, 0:n], start=True, stop=True)

            keep_warm(WARM)
            for h in range(HALVES):
                pe.wait_ge(s_x[h], 16)
                for net, done in ((0, s_gate_mm), (1, s_inner_mm)):
                    if h == 0:
                        pe.wait_ge(s_wn, K_IN * (net + 1))
                    for k in range(K_IN):
                        last = mm(bank(gate_bank(h, net), HP), wn[:, net, k], x_s[:, h, k], start=(k == 0),
                                  stop=(k == K_IN - 1))
                    last.then_inc(done, 1)
            pe.wait_ge(s_w3pe, 16)
            pe.wait_ge(s_stats, 16)
            pe.wait_ge(s_wqkvo, 16)

            def embed(h):
                pe.wait_ge(s_prod, h + 1)
                mm(bank(tok_bank(h), HP), w3pe_s[:, 0:EMB], prod[:, h], start=True, stop=True).then_inc(s_tok_mm, 1)

            def norm_center(use, h, b, rows):
                mm(bank(b, HT), center, rows, start=True, stop=True).then_inc(s_cen[use], 1)

            def norm_var(use, h, b):
                pe.wait_ge(s_sq[use], h + 1)
                pe.wait_ge(s_xc[use], h + 1)
                mm(bank(b, HT), mean, sq[:, use, h], start=True, stop=True).then_inc(s_var[use], 1)

            def center_tokens(h):
                pe.wait_ge(s_cls, 1)
                pe.wait_ge(s_X, h + 1)
                norm_center(0, h, cen_bank(h), X[:, h].rearrange("p i t -> p (i t)"))

            def project(h):
                pe.wait_ge(s_n1, h + 1)
                for c in range(3):
                    mm(bank(qkv_bank(h, c), HT), wqkvo_s[:, c], n1[:, h], start=True, stop=True).then_inc(s_qkv_mm, 1)

            keep_warm(WARM_START[0], cen_bank(1))
            embed(0)
            keep_warm(WARM_START[1], cen_bank(1))
            center_tokens(0)
            keep_warm(WARM_START[2], cen_bank(1))
            norm_var(0, 0, tok_bank(0))
            embed(1)
            center_tokens(1)
            keep_warm(WARM_START[3], cen_bank(0))
            project(0)
            norm_var(0, 1, tok_bank(1))
            keep_warm(WARM_START[4], cen_bank(0))
            project(1)

            def unit_place(n):
                return n // UNITS, UG * (n % UNITS)

            def unit_scores(n):
                h, g0 = unit_place(n)
                if n >= 2:
                    pe.wait_ge(s_sub, n - 1)
                if n % UNITS == 0:
                    pe.wait_ge(s_lq, h + 1)
                    pe.wait_ge(s_lk, (3, 5)[h])
                    pe.wait_ge(s_lkd, (1, 3)[h])
                q_h = q_l[:, h].rearrange("p t j -> p (t j)")
                k_h = k_l[:, h].rearrange("p i t j -> p i (t j)")
                for g in range(UG):
                    chunk = slice((g0 + g) * TOKENS, (g0 + g + 1) * TOKENS)
                    last = mm(scores(n)[:, g], q_h[:, chunk], k_h[:, :, chunk], start=True, stop=True)
                last.then_inc(s_score, 1)

            def unit_transposes(n):
                pe.wait_ge(s_exp, n + 1)
                if n >= 1:
                    pe.wait_ge(s_pTs, n)
                if n == 0:
                    pe.wait_ge(s_v1, 2)
                for g in range(UNIT):
                    last = nc.tensor.transpose(probTs[:, g // HI, g % HI], prob[:, n % 3, g], ident[0:TOKENS, 0:TOKENS])
                last.then_inc(s_pT, 1)

            def unit_context(n):
                h, g0 = unit_place(n)
                pe.wait_ge(s_pTs, n + 1)
                if n == UNITS:
                    pe.wait_ge(s_v1, 4)
                if n >= 1:
                    pe.wait_ge(s_ctxn, n)
                for g in range(UNIT):
                    last = mm(pv[:, g, 0:DH + 1], probT[:, n % 2, g], v1[:, h, g0 + g // HI, g % HI],
                              start=True, stop=True)
                last.then_inc(s_pv, 1)

            def values(h, part):
                if part == 0:
                    pe.wait_ge(s_lv, h + 1)
                if h == 1 and part == 1:
                    pe.wait_ge(s_v1, 3)
                v_h = v_l[:, h].rearrange("p t j -> p (t j)")
                for g in range(PART):
                    chunk = (part * PART + g) * TOKENS
                    last = nc.tensor.transpose(vT(h, part)[:, g], v_h[:, chunk:chunk + TOKENS], ident)
                last.then_inc(s_vT, 1)

            def context_images(h, part):
                pe.wait_ge(s_ctxn, h * UNITS + (part + 1) * UNITS // 2)
                if h == 1:
                    pe.wait_ge(s_pTs, ALL_UNITS)
                elif part == 0:
                    pe.wait_ge(s_v1, 4)
                else:
                    pe.wait_ge(s_ctxc, 1)
                for g in range(PART):
                    last = nc.tensor.transpose(ctxT(h, part)[:, g * TOKENS:(g + 1) * TOKENS],
                                               ctxn[:, h, part * PART + g].rearrange("p i d -> p (i d)"),
                                               ident[0:TOKENS, 0:TOKENS])
                last.then_inc(s_ctxT, 1)

            keep_warm(WARM_REGROUP)
            pe.wait_ge(s_qk, 4)
            pe.wait_ge(s_v, 2)
            unit_scores(0)
            unit_scores(1)
            keep_warm(WARM_KEYS)
            values(0, 0)
            values(0, 1)

            def attend_out(h):
                pe.wait_ge(s_ctxf[h], 16 * HI)
                if h == 0:
                    pe.wait_ge(s_ctxc, 2)
                else:
                    pe.wait_ge(s_route_step, 1)
                mm(bank(NORM_BANK, HT), wqkvo_s[:, 3], ctx_f[:, h].rearrange("p i t -> p (i t)"), start=True,
                   stop=True).then_inc(s_o_mm, 1)

            def center_attended(h):
                pe.wait_ge(s_y, h + 1)
                norm_center(1, h, NORM_BANK, y[:, h])

            def center_hidden(h):
                pe.wait_ge(s_XB, h + 1)
                pe.wait_ge(s_cgamma, 1)
                pe.wait_ge(s_lnv[1], h + 1)
                mm(bank(NORM_BANK, HT), center, XB[:, h], start=True, stop=False)
                if h == 0:
                    keep_warm(1, 0)
                pe.wait_ge(s_z, h + 1)
                mm(bank(NORM_BANK, HT), center_gamma[:], z[:, h], start=False, stop=True).then_inc(s_cen[2], 1)

            def gate_logits(h):
                pe.wait_ge(s_flat, h + 1)
                for i in range(HI):
                    last = mm(logits(h)[:, i], flat[:, h, i * TOKENS:(i + 1) * TOKENS], gates_s, start=True, stop=True)
                last.then_inc(s_lg_mm, 1)

            def pair(h, m):
                n = h * PAIRS + m
                before = [k for k in range(n) if PAIR_SLOTS[k] == PAIR_SLOTS[n]]
                if before:
                    pe.wait_ge(s_hid, before[-1] + 1)
                q = PAIR_ORDER[m]
                for ab, b in zip(range(2), pair_banks(n)):
                    last = mm(bank(b, HT), win_s[:, q // NK, NK * ab + q % NK], flat[:, h], start=True, stop=True)
                last.then_inc(s_ab, 1)

            def bias_out(h):
                pe.wait_ge(s_routeTf, h + 1)
                mm(bank(y_bank(h), HT), ebias_s, routeTf[:, h], start=True, stop=False)

            def shared_out(h):
                pe.wait_ge(s_hid, (h + 1) * PAIRS)
                for k in range(NK):
                    mm(bank(y_bank(h), HT), wso_s[:, k], hid[:, h, k], start=False, stop=False)

            def route_transposes(h):
                pe.wait_ge(s_route[h], 2)
                if h == 0:
                    pe.wait_ge(s_hid, 2)
                else:
                    pe.wait_ge(s_route_step, ROUTE_STEPS + 1)
                for i in range(HI):
                    last = nc.tensor.transpose(routeT_p(h)[:, i], route[:, h, i].rearrange("p a e -> p (a e)"),
                                               identb[0:TOKENS, 0:TOKENS])
                last.then_inc(s_routeT_mm, 1)

            def broadcast(h, e):
                if e == 0:
                    pe.wait_ge(s_routeT, h + 1)
                    pe.wait_ge(s_hid, 3)
                behind = [m for m in range(h * EXPERTS + e) if cb_bank(m % EXPERTS) == cb_bank(e)]
                if behind:
                    hb, eb = behind[-1] // EXPERTS, behind[-1] % EXPERTS
                    if eb in POOL_EXPERTS[hb]:
                        pe.wait_ge(s_cbs, pool_experts(hb, eb))
                    else:
                        pe.wait_ge(s_hsc, dve_experts(hb, eb))
                mm(bank(cb_bank(e), HT), selb[:, e], routeT[:, h], start=True, stop=True).then_inc(s_cb, 1)

            def expert_out(h, e):
                if e in POOL_EXPERTS[h]:
                    n = pool_experts(h, e)
                    pe.wait_ge(s_hsp, n)
                    src = hsp[:, n % 2]
                else:
                    n = dve_experts(h, e)
                    pe.wait_ge(s_hsc, n)
                    src = hsc[:, n % 3]
                for k in range(NK):
                    last = mm(bank(y_bank(h), HT), weo_s[:, e, k], src[:, k], start=False,
                              stop=(e == EXPERTS - 1 and k == NK - 1))
                last.then_inc(s_ehid, 1)

            for n in range(ALL_UNITS):
                if n >= 1:
                    keep_warm(1, 4, WARM_UNIT[n >= ALL_UNITS - 2])
                unit_transposes(n)
                if n + 2 < ALL_UNITS:
                    unit_scores(n + 2)
                if n == 1:
                    values(1, 0)
                if n == 2:
                    values(1, 1)
                if n == 3:
                    context_images(0, 0)
                if n == 4:
                    context_images(0, 1)
                if n == 6:
                    keep_warm(1, 0)
                    attend_out(0)
                if n == 7:
                    keep_warm(1, 0)
                    norm_var(1, 0, NORM_BANK)
                unit_context(n)
                if n == 6:
                    center_attended(0)
            context_images(1, 0)
            center_hidden(0)
            context_images(1, 1)
            keep_warm(WARM_TAIL[0], 0)
            norm_var(2, 0, NORM_BANK)
            keep_warm(WARM_TAIL[1], 0)
            pe.wait_ge(s_misc, 16)
            gate_logits(0)
            pe.wait_ge(s_win, 16)
            pe.wait_ge(s_wso, 16)
            pe.wait_ge(s_weo, 16)
            pe.wait_ge(s_selb, 1)
            pe.wait_ge(s_identb, 1)
            pe.wait_ge(s_ctxn, ALL_UNITS)
            pe.wait_ge(s_ctxc, 4)
            pair(0, 0)
            pair(0, 1)
            pair(0, 2)
            attend_out(1)
            keep_warm(WARM_ROUTE[0], y_bank(0))
            pair(0, 3)
            keep_warm(WARM_ROUTE[1], y_bank(0))
            center_attended(1)
            route_transposes(0)
            keep_warm(WARM_ROUTE[2], y_bank(0))
            broadcast(0, 0)
            broadcast(0, 1)
            norm_var(1, 1, NORM_BANK)
            bias_out(0)
            broadcast(0, 2)
            expert_out(0, 0)
            broadcast(0, 3)
            expert_out(0, 1)
            center_hidden(1)
            shared_out(0)
            broadcast(0, 4)
            norm_var(2, 1, NORM_BANK)
            broadcast(0, 5)
            expert_out(0, 2)
            expert_out(0, 3)
            gate_logits(1)
            pair(1, 0)
            broadcast(0, 6)
            expert_out(0, 4)
            pair(1, 1)
            broadcast(0, 7)
            expert_out(0, 5)
            expert_out(0, 6)
            pair(1, 2)
            expert_out(0, 7)
            route_transposes(1)
            broadcast(1, 0)
            pair(1, 3)
            broadcast(1, 1)
            bias_out(1)
            for e in range(EXPERTS):
                if e + 2 < EXPERTS:
                    broadcast(1, e + 2)
                expert_out(1, e)
                if e == 2:
                    shared_out(1)


def kernel(**inputs):
    import numpy as np
    import concourse.bacc as bacc
    from concourse.bass_utils import run_bass_kernel_spmd as run

    a = {k: np.asarray(v) for k, v in inputs.items()}

    def lay(x):
        return np.ascontiguousarray(x)

    px = a["x"].reshape(IMAGES, 8, 16, 8, 16).transpose(0, 1, 3, 2, 4).reshape(HALVES, HP, K_IN, EMB)
    patches = lay(px.transpose(0, 3, 2, 1))

    def tok_w(w):
        return w.T.reshape(K_IN, EMB, EMB).transpose(1, 0, 2)

    wtok = lay(np.stack([np.stack([tok_w(a[f"L0_tok_W{n}_w"]), tok_w(a[f"L0_tok_W{n}_sw"])], 1) for n in (1, 2)], 1))
    order = np.arange(EMB).reshape(CHUNKS, DH).T.reshape(-1)
    ei1, ei2 = a["L0_tok_eps_in1"].reshape(K_IN, EMB), a["L0_tok_eps_in2"].reshape(K_IN, EMB)
    cols = lay(np.stack([
        ei1[0], ei1[1], ei2[0], ei2[1], a["L0_tok_eps_out1"], a["L0_tok_eps_out2"], a["L0_tok_W1_b"], a["L0_tok_W2_b"],
        a["L0_tok_W1_sb"], a["L0_tok_W2_sb"], a["L0_tok_W3_b"], a["L0_attn_bq"][order], a["L0_attn_bk"][order],
        a["L0_attn_bv"][order], a["L0_attn_bo"], a["L0_attn_gamma"], a["L0_attn_beta"], a["L0_ffn_ln_scale"],
        a["L0_ffn_ln_bias"], a["L0_ffn_shared_out_b"], a["cls_tok"].reshape(-1)], 1))
    eob = lay(np.concatenate([a["L0_tok_eps_out1"], a["L0_tok_eps_out2"]]))
    pos = np.arange(PATCHES, dtype=np.float32)[:, None]
    div = np.exp(np.arange(0, EMB, 2, dtype=np.float32) * np.float32(-np.log(10000.0) / EMB)).astype(np.float32)
    ang = (pos * div).astype(np.float32)
    pe = np.stack([np.sin(ang), np.cos(ang)], -1).reshape(PATCHES, EMB).astype(np.float32)
    w3pe = lay(np.concatenate([a["L0_tok_W3_w"].T, pe.T], 1))
    eye = np.eye(EMB, dtype=np.float32)
    one_nth = np.full((EMB, EMB), 1.0 / EMB, np.float32)
    stats = lay(np.stack([eye, eye - one_nth, one_nth], 1))
    wqkvo = lay(np.stack([a["L0_attn_Wq"].T[:, order], a["L0_attn_Wk"].T[:, order], a["L0_attn_Wv"].T[:, order],
                          a["L0_attn_Wo"].T[order, :]], 1))
    win = lay(np.stack([a["L0_ffn_shared_in_w"].T.reshape(EMB, 4, EMB), a["L0_ffn_expert_in_w"].T.reshape(EMB, 4, EMB)], 1))
    wso = lay(a["L0_ffn_shared_out_w"].T.reshape(NK, EMB, EMB).transpose(1, 0, 2))
    weo = lay(a["L0_ffn_expert_out_weight"].reshape(EXPERTS, EMB, NK, EMB).transpose(3, 0, 2, 1))
    misc = np.zeros((EMB, MISC), np.float32)
    misc[:, M_GATES:M_GBIAS] = np.concatenate([a["L0_ffn_group_gate_w"], a["L0_ffn_expert_gate_w"]], 0).T
    tri = (np.arange(EG)[None, :] < np.arange(EG)[:, None]).astype(np.float32).reshape(-1)
    misc[0:TOKENS, M_GBIAS:M_EBIAS] = np.concatenate([a["L0_ffn_group_bias"], a["L0_ffn_expert_bias"], tri])
    misc[24:32, M_EBIAS:M_SEL] = a["L0_ffn_expert_out_bias"]
    for e in range(EXPERTS):
        misc[[e, EXPERTS + e, 2 * EXPERTS + e], M_SEL + e] = 1.0

    arrays = dict(cols=cols, eob=eob, patches=patches, wtok=wtok, w3pe=w3pe, stats=stats, wqkvo=wqkvo, win=win, wso=wso,
                  weo=weo, misc=misc)
    nc = bacc.Bacc("TRN2", target_bir_lowering=False, num_devices=1)
    args = [nc.dram_tensor(k, v.shape, F32, kind="ExternalInput").ap() for k, v in arrays.items()]
    out = nc.dram_tensor("out", (EMB, HALVES * HT), F32, kind="ExternalOutput").ap()
    vit_tower(nc, *args, out)
    r = run(nc, [arrays], core_ids=[0])
    return lay(r.results[0]["out"].T.reshape(IMAGES, TOKENS, EMB))
```
